# Optimizing a Trainium2 kernel written in Bass

```python
import numpy as np
import jax
import jax.numpy as jnp

def _softmax(x, axis=-1):
    return jax.nn.softmax(x, axis=axis)

def _gelu(x):
    return jax.nn.gelu(x, approximate=True)

def _silu(x):
    return jax.nn.silu(x)

def _sigmoid(x):
    return jax.nn.sigmoid(x)

def _layernorm(x, axis=-1, eps=1e-05):
    m = jnp.mean(x, axis=axis, keepdims=True)
    v = jnp.var(x, axis=axis, keepdims=True)
    return (x - m) / jnp.sqrt(v + eps)

def _scatter_add(tgt, idx, src, axis=0):
    return tgt.at[idx].add(src)

def _segment_sum(src, seg, n):
    return jax.ops.segment_sum(src, seg, n)
kernel_name = 'mk_adj_preln_d2_adj_r2_f375cf'

def setup_inputs(seed: int=0):
    np.random.seed(seed)
    _w = jnp.asarray

    def _rec_inputs():
        import jax
        import jax.numpy as jnp
        _gk = jax.random.key(seed)
        x = -0.0002928 + 1 * jax.random.normal(jax.random.fold_in(_gk, 1), (32, 256, 64), jnp.float32)
        _a = jax.random.bernoulli(jax.random.fold_in(_gk, 2), 0.0078125, (256, 256))
        _a = jnp.logical_or(_a, jnp.swapaxes(_a, -1, -2))
        _a = jnp.logical_or(_a, jnp.eye(256, dtype=bool))
        _af = _a.astype(jnp.float32)
        _af = _af * jax.random.uniform(jax.random.fold_in(_gk, 3), (256, 256), jnp.float32, 0.05, 0.000488281)
        adj = _af
        return (x, adj)
    x, adj = _rec_inputs()

    def _L0_gnn_setup():
        import jax, jax.numpy as jnp
        import numpy as np
        B, N, IN_SIZE, K, OUT = (32, 1024, 64, 2, 64)
        NUM_MATRICES = 2 * K + 1
        key = jax.random.key(seed)
        k1, k2, k3, k4 = jax.random.split(key, 4)
        inputs_and_state = jax.random.normal(k1, (B, N, IN_SIZE), dtype=jnp.float32)
        support0 = jax.random.uniform(k2, (N, N), dtype=jnp.float32) / N
        support1 = jax.random.uniform(k3, (N, N), dtype=jnp.float32) / N
        fan_in, fan_out = (IN_SIZE * NUM_MATRICES, OUT)
        std = 1.414 * np.sqrt(2.0 / (fan_in + fan_out))
        weight = jax.random.normal(k4, (fan_in, fan_out), dtype=jnp.float32) * std
        bias = jnp.zeros((OUT,), dtype=jnp.float32)
        return {'inputs_and_state': inputs_and_state, 'support0': support0, 'support1': support1, 'weight': weight, 'bias': bias}
    _L0_gnn_all = _L0_gnn_setup()
    _L0_gnn_in = {k: v for k, v in _L0_gnn_all.items() if k in ('weight', 'bias')}
    del _L0_gnn_all

    def _L1_gnn_setup():
        import jax, jax.numpy as jnp
        import numpy as np
        NEG_INF = -1e+16

        def gat_layer(x, graph, W, b):
            h = x @ W
            s = jnp.einsum('bnd,bmd->bnm', h, h) * graph
            s = jnp.where(s == 0.0, NEG_INF, s)
            a = jax.nn.softmax(s, axis=2)
            return jnp.einsum('bnm,bmd->bnd', a, h) + b
        key = jax.random.key(seed)
        k1, k2, k3, k4, k5, k6 = jax.random.split(key, 6)
        B, N, C_IN, HID, HEADS, C_OUT = (16, 512, 64, 128, 8, 64)
        flow_x = jax.random.normal(k1, (B, N, C_IN), dtype=jnp.float32)
        graph = jax.random.randint(k2, (N, N), 0, 2).astype(jnp.float32)
        Wh = jax.random.normal(k3, (HEADS, C_IN, HID), dtype=jnp.float32)
        bh = jax.random.normal(k4, (HEADS, HID), dtype=jnp.float32)
        W_out = jax.random.normal(k5, (HID * HEADS, C_OUT), dtype=jnp.float32)
        b_out = jax.random.normal(k6, (C_OUT,), dtype=jnp.float32)
        return {'flow_x': flow_x, 'graph': graph, 'Wh': Wh, 'bh': bh, 'W_out': W_out, 'b_out': b_out}
    _L1_gnn_all = _L1_gnn_setup()
    _L1_gnn_in = {k: v for k, v in _L1_gnn_all.items() if k in ('Wh', 'bh', 'W_out', 'b_out')}
    del _L1_gnn_all
    return {'x': x, 'adj': adj, 'L0_gnn_weight': _L0_gnn_in['weight'], 'L0_gnn_bias': _L0_gnn_in['bias'], 'L1_gnn_Wh': _L1_gnn_in['Wh'], 'L1_gnn_bh': _L1_gnn_in['bh'], 'L1_gnn_W_out': _L1_gnn_in['W_out'], 'L1_gnn_b_out': _L1_gnn_in['b_out']}

def reference(x, adj, L0_gnn_weight, L0_gnn_bias, L1_gnn_Wh, L1_gnn_bh, L1_gnn_W_out, L1_gnn_b_out):
    import jax
    import jax.numpy as jnp

    def _L0_gnn_ref(inputs_and_state, support0, support1, weight, bias):
        import jax, jax.numpy as jnp
        import numpy as np
        B, N, IN_SIZE, K, OUT = (32, 1024, 64, 2, 64)
        NUM_MATRICES = 2 * K + 1
        x0 = inputs_and_state
        x_stack = [x0]
        for support in (support0, support1):
            x1 = jnp.einsum('ij,bjk->bik', support, x0)
            x_stack.append(x1)
            x_prev, x_curr = (x0, x1)
            for _ in range(2, K + 1):
                x2 = 2.0 * jnp.einsum('ij,bjk->bik', support, x_curr) - x_prev
                x_stack.append(x2)
                x_prev, x_curr = (x_curr, x2)
        x_cat = jnp.concatenate(x_stack, axis=-1)
        out = jnp.einsum('bnf,fo->bno', x_cat, weight) + bias
        return out

    def _L1_gnn_ref(flow_x, graph, Wh, bh, W_out, b_out):
        import jax, jax.numpy as jnp
        import numpy as np
        NEG_INF = -1e+16

        def gat_layer(x, graph, W, b):
            h = x @ W
            s = jnp.einsum('bnd,bmd->bnm', h, h) * graph
            s = jnp.where(s == 0.0, NEG_INF, s)
            a = jax.nn.softmax(s, axis=2)
            return jnp.einsum('bnm,bmd->bnd', a, h) + b
        heads = jax.vmap(lambda W, b: gat_layer(flow_x, graph, W, b))(Wh, bh)
        H, B, N, D = heads.shape
        cat = jnp.moveaxis(heads, 0, 2).reshape(B, N, H * D)
        x = jax.nn.leaky_relu(cat, negative_slope=0.01)
        out = gat_layer(x, graph, W_out, b_out)
        return jax.nn.leaky_relu(out, negative_slope=0.01)
    h = jnp.maximum(_layernorm(x, axis=-1), 0.0)
    x = x + _L0_gnn_ref(h, adj, adj, L0_gnn_weight, L0_gnn_bias)
    h = jnp.maximum(_layernorm(x, axis=-1), 0.0)
    x = x + _L1_gnn_ref(h, adj, L1_gnn_Wh, L1_gnn_bh, L1_gnn_W_out, L1_gnn_b_out)
    return x

_drawn_inputs = setup_inputs


def setup_inputs(seed=0):
    import zlib

    import numpy as np

    out = dict(_drawn_inputs(seed))
    spreads = {'L0_gnn_bias': (0.0, 0.1)}
    factors = {'L1_gnn_b_out': 6.597}
    for name, (base, spread) in spreads.items():
        noise = np.random.default_rng([zlib.crc32(name.encode()), seed]).standard_normal(out[name].shape)
        drawn = base * np.exp(spread * noise) if base else spread * noise
        out[name] = jnp.asarray(drawn.astype(out[name].dtype))
    for name, factor in factors.items():
        out[name] = (out[name] * factor).astype(out[name].dtype)
    return out
```

```python
import concourse.bass as bass
from concourse import mybir
from contextlib import ExitStack

P = 128
NEG_INF = 1e16
SLOPE = 0.01
EPS = 1e-5

MIX = "mix"
SLOTS = [0, 1, 2, 3, 4, MIX, 5, 6, 7]
LAG_ST, LAG_AV, LAG_CT, LAG_WO = 2, 3, 4, 5


def graph_block(nc, x, adj, l0_w, l0_b, wh, bh, w_out, b_out, out):
    F32 = mybir.dt.float32
    ALU = mybir.AluOpType
    ACT = mybir.ActivationFunctionType
    AX = mybir.AxisListType

    B, N, K = x.shape
    HEADS, _, D = wh.shape
    T = N // P
    NM = l0_w.shape[0] // K
    CB = 8
    CHUNKS = B // CB
    PAIRS = CB // 2
    BK = CB * K

    ctx = ExitStack()
    with ctx:
        def sb(name, shape, dt=F32):
            return ctx.enter_context(nc.sbuf_tensor(name, shape, dt))

        def sem(name):
            return ctx.enter_context(nc.semaphore(name))

        bank = [ctx.enter_context(nc.psum_tensor(f"bank{i}", [P, 512], F32)) for i in range(8)]

        ident = sb("ident", [P, P])
        adj_raw = sb("adj_raw", [P, T, N])
        neg_adj = sb("neg_adj", [P, T, N])
        adj_t = sb("adj_t", [P, T, N])
        l0_raw = sb("l0_raw", [P, NM, K])
        l0_sum = sb("l0_sum", [P, K])
        conv_w = sb("conv_w", [P, 3, P])
        l0_bias = sb("l0_bias", [P, K])
        head_w = sb("head_w", [K, HEADS, D])
        head_b = sb("head_b", [P, HEADS, D])
        out_w = sb("out_w", [P, HEADS, K])
        out_b = sb("out_b", [P, K])
        eps = sb("eps", [P, 1])

        xs = sb("xs", [P, B, T, K])
        xb = sb("xb", [P, 2, CB, T, K])
        hn = sb("hn", [P, 2, T, CB, K])
        sq = sb("sq", [P, T, CB, K])
        ln_sum = sb("ln_sum", [P, CB * T])
        ln_mean = sb("ln_mean", [P, CB * T])
        ln_var = sb("ln_var", [P, CB * T])
        ln_std = sb("ln_std", [P, CB * T])
        ln_rs = sb("ln_rs", [P, CB * T])
        pair_t = sb("pair_t", [P, PAIRS, N])
        conv_c = sb("conv_c", [P, T, BK])
        conv_d = sb("conv_d", [P, T, BK])
        x_t = sb("x_t", [K, B, N])

        ht = sb("ht", [D, 2, N])
        hv = sb("hv", [P, 4, T, D + 1])
        u = sb("u", [P, 2, T, N])
        msk = sb("msk", [P, 2, T, N])
        nv = sb("nv", [P, 2, T, N])
        nmax = sb("nmax", [P, 2, T])
        dd = sb("dd", [P, 2, T, N])
        pt = sb("pt", [P, 2, T, N])
        rs = sb("rs", [P, 2, T])
        cat = sb("cat", [P, 2, T, D])
        catl = sb("catl", [P, 2, T, D])
        cat_t = sb("cat_t", [D, 2, N])

        m_ht = sb("m_ht", [K, N])
        m_hv = sb("m_hv", [P, T, K + 1])
        m_u = sb("m_u", [P, T, N])
        m_msk = sb("m_msk", [P, T, N])
        m_nv = sb("m_nv", [P, T, N])
        m_nmax = sb("m_nmax", [P, T])
        m_dd = sb("m_dd", [P, T, N])
        m_pt = sb("m_pt", [P, T, N])
        m_rs = sb("m_rs", [P, T])
        m_o = sb("m_o", [P, T, K])
        m_l = sb("m_l", [P, T, K])

        HT, HV, SC, ST, AV, CT, WO = bank[0], bank[1], bank[2], bank[3], bank[4], bank[5], bank[6]

        s_ld_x = [sem(f"x_loaded{c}") for c in range(CHUNKS)]
        s_ld_adj = sem("adj_loaded")
        s_ld_w = sem("weights_loaded")
        s_ident0 = sem("ident_zeroed")
        s_const = sem("constants_ready")
        s_w_mix = sem("conv_weights_steps")
        s_negadj = sem("neg_adj_ready")
        s_adj_tp = sem("adj_transposed")
        s_adj_t = sem("adj_t_in_sbuf")
        s_ln = sem("layernorm_step_vector")
        s_ln_m = sem("layernorm_mean")
        s_ln_sq = sem("layernorm_squares")
        s_ln_std = sem("layernorm_std")
        s_hn = sem("layernorm_ready")
        s_xb = sem("residual_with_bias")
        s_pt = sem("pairs_transposed")
        s_pt_sb = sem("pairs_in_sbuf")
        s_cm = sem("conv_matmuls")
        s_cm_sb = sem("conv_in_sbuf")
        s_x1 = sem("x1_ready")
        s_xt = sem("graphs_transposed")
        s_xt_sb = sem("graphs_t_in_sbuf")

        h_ht = sem("head_proj_done")
        h_ht_sb = sem("head_ht_in_sbuf")
        h_tr = sem("head_values_transposed")
        h_hv = sem("head_values_in_sbuf")
        h_sc = sem("head_scores_done")
        h_u = sem("head_scores_weighted")
        h_msk = sem("head_mask_done")
        h_nv = sem("head_masked_max_done")
        h_dd = sem("head_shifted_scores")
        h_st = sem("head_shifted_transposed")
        h_pt = sem("head_exp_done")
        h_av = sem("head_applied")
        h_rs = sem("head_reciprocal")
        h_cat = sem("head_normalised")
        h_lk = sem("head_leaky")
        h_ct = sem("head_cat_transposed")
        h_ct_sb = sem("head_cat_t_in_sbuf")
        h_wo = sem("head_projected_out")
        m_ht_sb = sem("mix_ht_in_sbuf")
        m_tr = sem("mix_values_transposed")
        m_hv_s = sem("mix_values_in_sbuf")
        m_sc = sem("mix_scores_done")
        m_us = sem("mix_scores_weighted")
        m_mk = sem("mix_mask_done")
        m_nvs = sem("mix_masked_max_done")
        m_dds = sem("mix_shifted_scores")
        m_st = sem("mix_shifted_transposed")
        m_pts = sem("mix_exp_done")
        m_av = sem("mix_applied")
        m_rss = sem("mix_reciprocal")
        m_os_first = sem("mix_output_read_out")
        m_os = sem("mix_output_steps")
        m_y = sem("mix_output_ready")
        s_out = sem("outputs_stored")
        s_apart = sem("apart")

        def slot(b, p, lag):
            q = p - lag
            g = b
            if q < 0:
                q += len(SLOTS)
                g = b - 1
            if SLOTS[q] == MIX:
                g = g - 1
            if type(g) is int and not 0 <= g < B:
                return None
            return SLOTS[q], g

        def heads(h, g):
            return g * HEADS + (h + 1)

        def mixes(g):
            return g + 2

        def rounds(eng, engine, body, mix_sems):
            for s in mix_sems:
                eng.sem_inc(s, 1)
            body(0)
            with nc.Fori(1, B, engines=[engine]) as b:
                body(b)
            body(B)

        def apart(eng):
            eng.sem_inc(s_apart, 1)

        block = ctx.enter_context(nc.Block())

        @block.sync
        def _(sp):
            xv = x.rearrange("b (p t) k -> p b (t k)", t=T)
            xd = xs[:, :, :, :].rearrange("p b t k -> p b (t k)")
            sp.dma_start(adj_raw[:, :, :], adj.rearrange("(p t) m -> p t m", t=T)).then_inc(s_ld_adj, 16)
            for c in range(CHUNKS):
                sp.dma_start(xd[:, c * CB:(c + 1) * CB, :], xv[:, c * CB:(c + 1) * CB, :]).then_inc(s_ld_x[c], 16)
            ov = out.rearrange("b (p t) k -> p b (t k)", t=T)

            def store(g):
                sp.wait_ge(m_y, g + 1)
                sp.dma_start(ov[:, bass.ds(g, 1), :], xd[:, bass.ds(g, 1), :]).then_inc(s_out, 16)

            with nc.Fori(0, B, engines=[mybir.EngineType.SP]) as g:
                store(g)
            sp.wait_ge(s_out, 16 * B)

        @block.gpsimd
        def _(pool):
            lw = l0_w.rearrange("(m k) o -> k m o", k=K)
            for r in range(2):
                pool.dma_start(l0_raw[r * K:(r + 1) * K, :, :], lw).then_inc(s_ld_w, 16)
            pool.dma_start(l0_bias[:, :], l0_b.partition_broadcast(P)).then_inc(s_ld_w, 16)
            pool.dma_start(head_w[:, :, :], wh.rearrange("h k d -> k h d")).then_inc(s_ld_w, 16)
            pool.dma_start(head_b[:, :, :], bh.partition_broadcast(P)).then_inc(s_ld_w, 16)
            pool.dma_start(out_w[:, :, :], w_out.rearrange("(h d) o -> d h o", d=D)).then_inc(s_ld_w, 16)
            pool.dma_start(out_b[:, :], b_out.partition_broadcast(P)).then_inc(s_ld_w, 16)
            pool.memset(ident[:, :], 0.0).then_inc(s_ident0, 1)
            pool.memset(conv_w[:, :, :], 0.0).then_inc(s_const, 1)
            pool.memset(eps[:, :], EPS).then_inc(s_const, 1)
            pool.memset(hv[:, :, :, D:D + 1], 1.0).then_inc(s_const, 1)
            pool.memset(m_hv[:, :, K:K + 1], 1.0).then_inc(s_const, 1)
            pool.wait_ge(s_ident0, 1)
            pool.affine_select(out=ident[:, :], in_=ident[:, :], compare_op=ALU.not_equal, fill=1.0,
                               base=0, pattern=[[-1, P]], channel_multiplier=1).then_inc(s_const, 1)
            pool.wait_ge(s_ld_w, 7 * 16)
            for c in range(CHUNKS):
                pool.wait_ge(s_ld_x[c], 16)
                if c >= 2:
                    pool.wait_ge(s_x1, T * (c - 1))
                pool.tensor_tensor(xb[:, c % 2, :, :, :].rearrange("p b t k -> p (b t) k"),
                                   xs[:, c * CB:(c + 1) * CB, :, :].rearrange("p b t k -> p (b t) k"),
                                   l0_bias[:, :].unsqueeze(1).broadcast_to([P, CB * T, K]),
                                   ALU.add).then_inc(s_xb, 1)

            def shift(b):
                for p in range(len(SLOTS)):
                    now = slot(b, p, 0)
                    if now is None:
                        continue
                    h, g = now
                    if h == MIX:
                        pool.wait_ge(m_nvs, mixes(g))
                        apart(pool)
                        for t in range(T):
                            last = pool.tensor_scalar(m_dd[:, t, :], m_nv[:, t, :], -1.0, m_nmax[:, t:t + 1],
                                                      ALU.mult, ALU.add)
                        last.then_inc(m_dds, 1)
                        continue
                    pool.wait_ge(h_nv, heads(h, g))
                    if not (type(g) is int and heads(h, g) <= 2):
                        pool.wait_ge(h_st, heads(h, g) - 2)
                    apart(pool)
                    for t in range(T):
                        last = pool.tensor_scalar(dd[:, h % 2, t, :], nv[:, h % 2, t, :], -1.0,
                                                  nmax[:, h % 2, t:t + 1], ALU.mult, ALU.add)
                    last.then_inc(h_dd, 1)

            rounds(pool, mybir.EngineType.Pool, shift, [m_dds])

        @block.scalar
        def _(act):
            def ln_act(n):
                act.wait_ge(s_ln, 4 * n + 2)
                act.activation(sq[:, :, :, :], hn[:, n % 2, :, :, :], ACT.Square).then_inc(s_ln_sq, 1)
                act.wait_ge(s_ln, 4 * n + 3)
                act.activation(ln_std[:, :], ln_var[:, :], ACT.Sqrt, scale=1.0 / K, bias=eps[:, :]).then_inc(s_ln_std, 1)

            def adj_copy():
                act.wait_ge(s_adj_tp, 1)
                act.activation(adj_t[:, :, :].rearrange("p t n -> p (t n)"), bank[0][:, :], ACT.Copy).then_inc(s_adj_t, 1)

            def conv_act(c):
                for i in range(2):
                    act.wait_ge(s_pt, 2 * c + i + 1)
                    if c >= 1 and i == 0:
                        act.wait_ge(s_cm, 3 * T * c)
                    act.activation(pair_t[:, 2 * i:2 * i + 2, :].rearrange("p a n -> p (a n)"), bank[i][:, :],
                                   ACT.Copy).then_inc(s_pt_sb, 1)
                for t in range(T):
                    act.wait_ge(s_cm, 3 * T * c + t + 1)
                    act.activation(conv_c[:, t, :], bank[2 + t][:, :], ACT.Copy).then_inc(s_cm_sb, 1)
                for t in range(T):
                    act.wait_ge(s_cm, 3 * T * c + T + t + 1)
                    act.activation(conv_d[:, t, :], bank[4 + t][:, :], ACT.Copy).then_inc(s_cm_sb, 1)

            act.wait_ge(s_const, 5)
            adj_copy()
            ln_act(0)
            ln_act(1)
            for c in range(CHUNKS):
                conv_act(c)
                if c + 2 < CHUNKS:
                    ln_act(c + 2)
            ln_act(CHUNKS)
            ln_act(CHUNKS + 1)
            for i in range(B // 2):
                act.wait_ge(s_xt, i + 1)
                act.activation(x_t[:, 2 * i:2 * i + 2, :].rearrange("k b n -> k (b n)"), bank[i % 2][0:K, :],
                               ACT.Copy).then_inc(s_xt_sb, 1)
                if i % PAIRS == PAIRS - 1 and i // PAIRS + 2 < CHUNKS:
                    ln_act(CHUNKS + i // PAIRS + 2)

            def attend(b):
                for p in range(len(SLOTS)):
                    now, st, av, ct = (slot(b, p, k) for k in (0, LAG_ST, LAG_AV, LAG_CT))
                    if now is not None and now[0] == MIX:
                        act.wait_ge(h_wo, heads(HEADS - 1, now[1]))
                        act.activation(m_ht[:, :], WO[0:K, 0:N], ACT.Copy).then_inc(m_ht_sb, 1)
                    elif now is not None:
                        h, g = now
                        act.wait_ge(h_ht, heads(h, g))
                        if not (type(g) is int and heads(h, g) <= 2):
                            act.wait_ge(h_sc, heads(h, g) - 2)
                        act.activation(ht[:, h % 2, :], HT[:, 0:N], ACT.Copy).then_inc(h_ht_sb, 1)
                    if st is not None:
                        h, g = st
                        if h == MIX:
                            act.wait_ge(m_st, mixes(g))
                            act.activation(m_pt[:, :, :].rearrange("p t n -> p (t n)"), ST[:, :], ACT.Exp).then_inc(m_pts, 1)
                        else:
                            act.wait_ge(h_st, heads(h, g))
                            if not (type(g) is int and heads(h, g) <= 2):
                                act.wait_ge(h_av, heads(h, g) - 2)
                            act.activation(pt[:, h % 2, :, :].rearrange("p t n -> p (t n)"), ST[:, :], ACT.Exp)\
                               .then_inc(h_pt, 1)
                    if av is not None and av[0] != MIX:
                        h, g = av
                        act.wait_ge(h_rs, heads(h, g))
                        if not (type(g) is int and heads(h, g) <= 2):
                            act.wait_ge(h_lk, heads(h, g) - 2)
                        for t in range(T):
                            last = act.activation(cat[:, h % 2, t, :], AV[:, t * (D + 1):t * (D + 1) + D], ACT.Copy,
                                                  scale=rs[:, h % 2, t:t + 1])
                        last.then_inc(h_cat, 1)
                    if ct is not None and ct[0] != MIX:
                        h, g = ct
                        act.wait_ge(h_ct, heads(h, g))
                        if not (type(g) is int and heads(h, g) <= 2):
                            act.wait_ge(h_wo, heads(h, g) - 2)
                        act.activation(cat_t[:, h % 2, :], CT[:, 0:N], ACT.Copy).then_inc(h_ct_sb, 1)

            rounds(act, mybir.EngineType.Activation, attend, [m_ht_sb, m_pts])

        @block.vector
        def _(dve):
            dve.wait_ge(s_ld_w, 7 * 16)
            dve.wait_ge(s_const, 5)
            dve.tensor_tensor(l0_sum[:, :], l0_raw[:, 2, :], l0_raw[:, 4, :], ALU.add).then_inc(s_w_mix, 1)
            dve.wait_ge(s_w_mix, 1)
            for r in range(2):
                q = slice(r * K, (r + 1) * K)
                dve.tensor_tensor(conv_w[q, 0, q], l0_raw[q, 0, :], l0_sum[q, :], ALU.subtract)
                dve.tensor_tensor(conv_w[q, 1, q], l0_raw[q, 1, :], l0_raw[q, 3, :], ALU.add)
                dve.tensor_scalar(conv_w[q, 2, q], l0_sum[q, :], 2.0, None, ALU.mult).then_inc(s_w_mix, 1)
            dve.wait_ge(s_ld_adj, 16)
            for t in range(T):
                last = dve.tensor_scalar(neg_adj[:, t, :].rearrange("p (s q) -> p s q", s=T),
                                         adj_raw[:, t, :].rearrange("p (q s) -> p s q", s=T), -1.0, None, ALU.mult)
            last.then_inc(s_negadj, 1)

            def layernorm(n, c):
                src = xs[:, c * CB:(c + 1) * CB, :, :].rearrange("p b t k -> p t b k")
                dst = hn[:, n % 2, :, :, :].rearrange("p t b k -> p (t b) k")
                sqv = sq[:, :, :, :].rearrange("p t b k -> p (t b) k")

                def wide(a):
                    return a[:, :].unsqueeze(2).broadcast_to([P, CB * T, K])

                dve.tensor_reduce(ln_sum[:, :].rearrange("p (t b) -> p t b", t=T), src, AX.X, ALU.add).then_inc(s_ln, 1)
                dve.wait_ge(s_ln, 4 * n + 1)
                dve.tensor_scalar(ln_mean[:, :], ln_sum[:, :], 1.0 / K, None, ALU.mult).then_inc(s_ln_m, 1)
                dve.wait_ge(s_ln_m, n + 1)
                dve.tensor_tensor(hn[:, n % 2, :, :, :], src,
                                  wide(ln_mean).rearrange("p (t b) k -> p t b k", t=T), ALU.subtract).then_inc(s_ln, 1)
                dve.wait_ge(s_ln_sq, n + 1)
                dve.tensor_reduce(ln_var[:, :], sqv, AX.X, ALU.add).then_inc(s_ln, 1)
                dve.wait_ge(s_ln_std, n + 1)
                dve.reciprocal(ln_rs[:, :], ln_std[:, :]).then_inc(s_ln, 1)
                dve.wait_ge(s_ln, 4 * n + 4)
                dve.scalar_tensor_tensor(dst, dst, 0.0, wide(ln_rs), ALU.max, ALU.mult).then_inc(s_hn, 1)

            def first_norm(c):
                dve.wait_ge(s_ld_x[c], 16)
                if c >= 2:
                    dve.wait_ge(s_pt, 2 * (c - 1))
                layernorm(c, c)

            first_norm(0)
            first_norm(1)
            for c in range(CHUNKS):
                for t in range(T):
                    dve.wait_ge(s_cm, 3 * T * c + 2 * T + t + 1)
                    dve.wait_ge(s_xb, c + 1)
                    dve.tensor_tensor(xs[:, c * CB:(c + 1) * CB, t, :],
                                      bank[6 + t][:, :].rearrange("p (b k) -> p b k", b=CB),
                                      xb[:, c % 2, :, t, :], ALU.add).then_inc(s_x1, 1)
                if c + 2 < CHUNKS:
                    first_norm(c + 2)
            for c in range(CHUNKS):
                dve.wait_ge(s_x1, T * (c + 1))
                if c >= 2:
                    dve.wait_ge(s_xt, PAIRS * (c - 1))
                layernorm(CHUNKS + c, c)

            def weigh(scores, u_, msk_, nv_, nmax_, s_u, s_m, s_n, count):
                dve.tensor_tensor(u_, scores, neg_adj[:, :, :].rearrange("p t n -> p (t n)"), ALU.mult).then_inc(s_u, 1)
                dve.wait_ge(s_u, count)
                dve.tensor_scalar(msk_, u_, 0.0, NEG_INF, ALU.is_equal, ALU.mult).then_inc(s_m, 1)
                dve.wait_ge(s_m, count)
                apart(dve)
                for t in range(T):
                    q = slice(t * N, (t + 1) * N)
                    last = dve.tensor_tensor_reduce(nv_[:, q], msk_[:, q], u_[:, q], 1.0, 3e38, ALU.add, ALU.min,
                                                    nmax_[:, t:t + 1])
                last.then_inc(s_n, 1)

            def attend(b):
                for p in range(len(SLOTS)):
                    now, av = (slot(b, p, k) for k in (0, LAG_AV))
                    if av is not None:
                        h, g = av
                        if h == MIX:
                            dve.wait_ge(m_av, mixes(g))
                            dve.reciprocal(m_rs[:, :], AV[:, K:T * (K + 1):K + 1]).then_inc(m_rss, 1)
                            dve.wait_ge(m_rss, mixes(g))
                            for t in range(T):
                                last = dve.scalar_tensor_tensor(m_o[:, t, :], AV[:, t * (K + 1):t * (K + 1) + K],
                                                                m_rs[:, t:t + 1], out_b[:, :], ALU.mult, ALU.add)
                            last.then_inc(m_os_first, 1)
                            dve.wait_ge(m_os_first, mixes(g))
                            dve.scalar_tensor_tensor(m_l[:, :, :], m_o[:, :, :], SLOPE, m_o[:, :, :],
                                                     ALU.mult, ALU.max).then_inc(m_os, 1)
                            dve.wait_ge(m_os, mixes(g))
                            here = xs[:, bass.ds(g, 1), :, :].rearrange("p b t k -> p (b t) k")
                            dve.tensor_tensor(here, m_l[:, :, :], here, ALU.add).then_inc(m_y, 1)
                        else:
                            dve.wait_ge(h_av, heads(h, g))
                            if not (type(g) is int and heads(h, g) <= 2):
                                dve.wait_ge(h_cat, heads(h, g) - 2)
                            dve.reciprocal(rs[:, h % 2, :], AV[:, D:T * (D + 1):D + 1]).then_inc(h_rs, 1)
                    if now is not None:
                        h, g = now
                        if h == MIX:
                            dve.wait_ge(m_tr, mixes(g))
                            dve.tensor_copy(m_hv[:, :, 0:K], HV[:, 0:T * K].rearrange("p (t k) -> p t k", t=T)).then_inc(m_hv_s, 1)
                        else:
                            dve.wait_ge(h_tr, heads(h, g))
                            if not (type(g) is int and heads(h, g) <= 4):
                                dve.wait_ge(h_av, heads(h, g) - 4)
                            dve.tensor_tensor(hv[:, h % 4, :, 0:D], HV[:, 0:T * D].rearrange("p (t d) -> p t d", t=T),
                                              head_b[:, h, :].unsqueeze(1).broadcast_to([P, T, D]),
                                              ALU.add).then_inc(h_hv, 1)
                    if av is not None and av[0] != MIX:
                        h, g = av
                        dve.wait_ge(h_cat, heads(h, g))
                        if not (type(g) is int and heads(h, g) <= 2):
                            dve.wait_ge(h_ct, heads(h, g) - 2)
                        dve.scalar_tensor_tensor(catl[:, h % 2, :, :], cat[:, h % 2, :, :], SLOPE, cat[:, h % 2, :, :],
                                                 ALU.mult, ALU.max).then_inc(h_lk, 1)
                    if now is not None:
                        h, g = now
                        if h == MIX:
                            dve.wait_ge(m_sc, mixes(g))
                            dve.wait_ge(m_dds, mixes(g) - 1)
                            flat = [a[:, :, :].rearrange("p t n -> p (t n)") for a in (m_u, m_msk, m_nv)]
                            weigh(SC[:, :], *flat, m_nmax, m_us, m_mk, m_nvs, mixes(g))
                        else:
                            dve.wait_ge(h_sc, heads(h, g))
                            if not (type(g) is int and heads(h, g) <= 2):
                                dve.wait_ge(h_dd, heads(h, g) - 2)
                            flat = [a[:, h % 2, :, :].rearrange("p t n -> p (t n)") for a in (u, msk, nv)]
                            weigh(SC[:, :], *flat, nmax[:, h % 2, :], h_u, h_msk, h_nv, heads(h, g))

            rounds(dve, mybir.EngineType.DVE, attend, [m_hv_s, m_us, m_mk, m_nvs, m_rss, m_os_first, m_os])

        @block.tensor
        def _(pe):
            pe.wait_ge(s_const, 5)
            pe.wait_ge(s_ld_adj, 16)
            for s in range(T):
                for t in range(T):
                    last = pe.transpose(bank[0][:, s * N + t * P:s * N + (t + 1) * P],
                                        adj_raw[:, t, s:N:T], ident[:, :])
            last.then_inc(s_adj_tp, 1)

            def conv(c):
                pe.wait_ge(s_hn, c + 1)
                for i in range(2):
                    if c == 0 and i == 0:
                        pe.wait_ge(s_adj_t, 1)
                    if c >= 1:
                        pe.wait_ge(s_pt_sb, 2 * (c - 1) + i + 1)
                    for a in range(2):
                        for t in range(T):
                            g = 2 * (2 * i + a)
                            last = pe.transpose(bank[i][:, a * N + t * P:a * N + (t + 1) * P],
                                                hn[:, c % 2, t, g:g + 2, :].rearrange("p b k -> p (b k)"), ident[:, :])
                    last.then_inc(s_pt, 1)
                for step, (source, w) in enumerate([(None, 2), (conv_c, 1), (conv_d, 0)]):
                    for t in range(T):
                        out_bank = bank[2 + 2 * step + t]
                        if step < 2 and c >= 1:
                            pe.wait_ge(s_cm_sb, 2 * T * (c - 1) + T * step + t + 1)
                        if step == 2 and c >= 1:
                            pe.wait_ge(s_x1, T * (c - 1) + t + 1)
                        if source is not None:
                            pe.wait_ge(s_cm_sb, 2 * T * c + T * step)
                            for m in range(T):
                                pe.matmul(out_bank[:, :], adj_t[:, m, t * P:(t + 1) * P], source[:, m, :],
                                          start=(m == 0), stop=False, skip_group_check=True)
                        for a in range(PAIRS):
                            if step == 0:
                                pe.wait_ge(s_pt_sb, 2 * c + a // 2 + 1)
                            if step == 0 and c == 0:
                                pe.wait_ge(s_w_mix, 3)
                            last = pe.matmul(out_bank[:, a * P:(a + 1) * P], pair_t[:, a, t * P:(t + 1) * P],
                                             conv_w[:, w, :], start=(source is None and a == 0),
                                             stop=(a == PAIRS - 1), skip_group_check=True)
                        last.then_inc(s_cm, 1)

            for c in range(CHUNKS):
                conv(c)
            for i in range(B // 2):
                c = i // PAIRS
                pe.wait_ge(s_hn, CHUNKS + c + 1)
                if i >= 2:
                    pe.wait_ge(s_xt_sb, i - 1)
                for a in range(2):
                    for t in range(T):
                        g = 2 * (i % PAIRS) + a
                        last = pe.transpose(bank[i % 2][0:K, a * N + t * P:a * N + (t + 1) * P],
                                            hn[:, (CHUNKS + c) % 2, t, g, :], ident[:, :])
                last.then_inc(s_xt, 1)
            pe.wait_ge(s_xt_sb, B // 2)
            pe.wait_ge(s_negadj, 1)

            def free(b, p, lag, s_head, s_mix):
                for back in (lag + 1, lag + 2):
                    user = slot(b, p, back)
                    if user is not None and user[0] == MIX:
                        pe.wait_ge(s_mix, mixes(user[1]))
                    elif user is not None:
                        pe.wait_ge(s_head, heads(*user))
                        return

            def attend(b):
                for p in range(len(SLOTS)):
                    now, st, av, ct, wo = (slot(b, p, k) for k in (0, LAG_ST, LAG_AV, LAG_CT, LAG_WO))
                    if now is not None and now[0] != MIX:
                        h, g = now
                        if not (type(g) is int and heads(h, g) <= 1):
                            pe.wait_ge(h_ht_sb, heads(h, g) - 1)
                        apart(pe)
                        pe.matmul(HT[:, 0:N], head_w[:, h, :],
                                  x_t[:, bass.ds(g, 1), :].rearrange("k b n -> k (b n)"),
                                  start=True, stop=True).then_inc(h_ht, 1)
                    if st is not None:
                        h, g = st
                        mix = h == MIX
                        pe.wait_ge(m_dds if mix else h_dd, mixes(g) if mix else heads(h, g))
                        free(b, p, LAG_ST, h_pt, m_pts)
                        src = m_dd if mix else dd[:, h % 2, :, :]
                        for s in range(T):
                            for t in range(T):
                                last = pe.transpose(ST[:, s * N + t * P:s * N + (t + 1) * P],
                                                    src[:, t, s * P:(s + 1) * P], ident[:, :])
                        last.then_inc(m_st if mix else h_st, 1)
                    if av is not None:
                        h, g = av
                        mix = h == MIX
                        w = (K if mix else D) + 1
                        pe.wait_ge(m_pts if mix else h_pt, mixes(g) if mix else heads(h, g))
                        pe.wait_ge(m_hv_s if mix else h_hv, mixes(g) if mix else heads(h, g))
                        free(b, p, LAG_AV, h_cat, m_os_first)
                        prob = m_pt if mix else pt[:, h % 2, :, :]
                        val = m_hv if mix else hv[:, h % 4, :, :]
                        for t in range(T):
                            for s in range(T):
                                last = pe.matmul(AV[:, t * w:(t + 1) * w], prob[:, s, t * P:(t + 1) * P],
                                                 val[:, s, :], start=(s == 0), stop=(s == T - 1))
                        last.then_inc(m_av if mix else h_av, 1)
                    if now is not None:
                        h, g = now
                        mix = h == MIX
                        w = K if mix else D
                        src = m_ht[:, :] if mix else ht[:, h % 2, :]
                        pe.wait_ge(m_ht_sb if mix else h_ht_sb, mixes(g) if mix else heads(h, g))
                        free(b, p, 0, h_hv, m_hv_s)
                        apart(pe)
                        for t in range(T):
                            last = pe.transpose(HV[:, t * w:(t + 1) * w], src[:, t * P:(t + 1) * P], ident[0:w, 0:w])
                        last.then_inc(m_tr if mix else h_tr, 1)
                        free(b, p, 0, h_u, m_us)
                        for t in range(T):
                            last = pe.matmul(SC[:, t * N:(t + 1) * N], src[:, t * P:(t + 1) * P], src,
                                             start=True, stop=True)
                        last.then_inc(m_sc if mix else h_sc, 1)
                    if ct is not None and ct[0] != MIX:
                        h, g = ct
                        pe.wait_ge(h_lk, heads(h, g))
                        if not (type(g) is int and heads(h, g) <= 1):
                            pe.wait_ge(h_ct_sb, heads(h, g) - 1)
                        for t in range(T):
                            last = pe.transpose(CT[:, t * P:(t + 1) * P], catl[:, h % 2, t, :], ident[:, :])
                        last.then_inc(h_ct, 1)
                    if wo is not None and wo[0] != MIX:
                        h, g = wo
                        pe.wait_ge(h_ct_sb, heads(h, g))
                        if h == 0:
                            pe.wait_ge(m_ht_sb, mixes(g) - 1)
                        pe.matmul(WO[0:K, 0:N], out_w[:, h, :], cat_t[:, h % 2, :],
                                  start=(h == 0), stop=(h == HEADS - 1), skip_group_check=True).then_inc(h_wo, 1)

            rounds(pe, mybir.EngineType.PE, attend, [m_tr, m_sc, m_st, m_av])


_INS = ["x", "adj", "L0_gnn_weight", "L0_gnn_bias", "L1_gnn_Wh", "L1_gnn_bh", "L1_gnn_W_out", "L1_gnn_b_out"]
_OUTS = [((32, 256, 64), "float32")]


def kernel(**inputs):
    import numpy as _np
    import concourse.bacc as _bacc
    from concourse import mybir as _mybir
    from concourse.bass_utils import run_bass_kernel_spmd as _run

    nc = _bacc.Bacc("TRN2", target_bir_lowering=False, num_devices=1)
    arrays, args = {}, []
    for name in _INS:
        a = _np.ascontiguousarray(inputs[name])
        arrays[f"in_{name}_dram"] = a
        args.append(nc.dram_tensor(f"in_{name}_dram", a.shape, _mybir.dt.from_np(a.dtype), kind="ExternalInput").ap())
    for i, (shape, dtype) in enumerate(_OUTS):
        dt = _mybir.dt.from_np(_np.dtype(dtype))
        args.append(nc.dram_tensor(f"out_{i}_dram", shape, dt, kind="ExternalOutput").ap())
    graph_block(nc, *args)
    r = _run(nc, [arrays], core_ids=[0])
    got = tuple(r.results[0][f"out_{i}_dram"] for i in range(len(_OUTS)))
    return got[0]
```

```python
import concourse.bass as bass
from concourse import mybir
from contextlib import ExitStack

P = 128
NEG_INF = 1e16
SLOPE = 0.01
EPS = 1e-5

MIX = "mix"
SLOTS = [0, 1, 2, 3, 4, 5, MIX, 6, 7]
LAG = dict(y=0, y_hi=0, y_lo=0, scores=0, values=1, weighted=1, mask=1, masked=2, shifted=1, transposed=2,
           exp=2, applied=3, reciprocal=3, normalised=3, part_hi=4, part_lo=3, back=4, back_sb=5,
           projected=5, biased=5, leaky=6, out_hi=6, out_lo=5, out=6)


def graph_block(nc, x, adj, l0_w, l0_b, wh, bh, w_out, b_out, out):
    F32 = mybir.dt.float32
    F32R = mybir.dt.float32r
    ALU = mybir.AluOpType
    ACT = mybir.ActivationFunctionType
    AX = mybir.AxisListType

    B, N, K = x.shape
    HEADS, _, D = wh.shape
    T = N // P
    NM = l0_w.shape[0] // K
    CB = 8
    CHUNKS = B // CB
    PAIRS = CB // 2
    BK = CB * K

    ctx = ExitStack()
    with ctx:
        def sb(name, shape, dt=F32):
            return ctx.enter_context(nc.sbuf_tensor(name, shape, dt))

        def sem(name):
            return ctx.enter_context(nc.semaphore(name))

        bank = [ctx.enter_context(nc.psum_tensor(f"bank{i}", [P, 512], F32)) for i in range(8)]

        ident = sb("ident", [P, P])
        adj_raw = sb("adj_raw", [P, T, N])
        neg_adj = sb("neg_adj", [P, T, N])
        adj_t = sb("adj_t", [P, T, N])
        l0_raw = sb("l0_raw", [P, NM, K])
        l0_sum = sb("l0_sum", [P, K])
        conv_w = sb("conv_w", [P, 3, P])
        l0_bias = sb("l0_bias", [P, K])
        head_w = sb("head_w", [P, HEADS, D])
        head_wt = sb("head_wt", [D, HEADS, 2, K])
        head_b_rows = sb("head_b_rows", [HEADS, D])
        head_b = sb("head_b", [D, HEADS])
        head_hi = sb("head_hi", [P, HEADS, D], F32R)
        head_lo = sb("head_lo", [P, HEADS, D], F32R)
        gram = sb("gram", [P, HEADS, P], F32R)
        out_w = sb("out_w", [P, HEADS, K])
        out_parts = sb("out_parts", [P, HEADS, 2, K], F32R)
        out_b = sb("out_b", [P, K])
        eps = sb("eps", [P, 1])

        xs = sb("xs", [P, B, T, K])
        xb = sb("xb", [P, 2, CB, T, K])
        hn = sb("hn", [P, 2, T, CB, K])
        sq = sb("sq", [P, T, CB, K])
        ln_sum = sb("ln_sum", [P, CB * T])
        ln_mean = sb("ln_mean", [P, CB * T])
        ln_var = sb("ln_var", [P, CB * T])
        ln_std = sb("ln_std", [P, CB * T])
        ln_rs = sb("ln_rs", [P, CB * T])
        pair_t = sb("pair_t", [P, PAIRS, N])
        conv_cd = sb("conv_cd", [P, 2, T, BK])
        conv_c, conv_d = conv_cd[:, 0, :, :], conv_cd[:, 1, :, :]
        z_two = [conv_cd[:, :, :, :].rearrange("p a t (b k) -> p (a t b k)", k=K),
                 xb[:, :, :, :, :].rearrange("p a b t k -> p (a b t k)")]
        z_two = [a.rearrange("p (t b r k) -> p t b r k", t=T, b=CB, r=2) for a in z_two]
        z = sb("z", [P, B, T, K + 1])
        zt_hi = sb("zt_hi", [P, B, N], F32R)
        zt_lo = sb("zt_lo", [P, B, N], F32R)

        u = sb("u", [P, 3, T, N])
        msk = sb("msk", [P, T, N])
        nv = sb("nv", [P, 3, T, N])
        nmax = sb("nmax", [P, 3, T])
        pt = sb("pt", [P, 3, T, N])
        rs = sb("rs", [P, 3, T])
        pz = sb("pz", [P, 3, T, K])
        y = sb("y", [P, 2, N], F32R)
        pz_parts = sb("pz_parts", [P, 2, T, 2, K], F32R)
        pzt = sb("pzt", [P, 2, N], F32R)
        cat_raw = sb("cat_raw", [D, 2, N])
        cat = sb("cat", [D, 2, N])
        cat_hi = sb("cat_hi", [D, 2, N], F32R)
        cat_lo = sb("cat_lo", [D, 2, N], F32R)
        m_parts = sb("m_parts", [K, 2, N])
        m_ht = sb("m_ht", [K, N])
        m_hv = sb("m_hv", [P, T, K + 1])
        m_o = sb("m_o", [P, T, K])
        m_l = sb("m_l", [P, T, K])

        Y, HV, SC, ST, AV, CT, WO, ZT = bank

        s_ld_x = [sem(f"x_loaded{c}") for c in range(CHUNKS)]
        s_ld_adj = sem("adj_loaded")
        s_ld_w = sem("weights_loaded")
        s_ident0 = sem("ident_zeroed")
        s_const = sem("constants_ready")
        s_w_mix = sem("conv_weights_steps")
        s_negadj = sem("neg_adj_ready")
        s_adj_tp = sem("adj_transposed")
        s_adj_t = sem("adj_t_in_sbuf")
        s_ln = sem("layernorm_step_vector")
        s_ln_m = sem("layernorm_mean")
        s_ln_sq = sem("layernorm_squares")
        s_ln_std = sem("layernorm_std")
        s_hn = sem("layernorm_ready")
        s_xb = sem("residual_with_bias")
        s_pt = sem("pairs_transposed")
        s_pt_sb = sem("pairs_in_sbuf")
        s_cm = sem("conv_matmuls")
        s_cm_sb = sem("conv_in_sbuf")
        s_x1 = sem("x1_ready")
        s_two = sem("layernorm_doubled")
        s_xt = sem("graphs_transposed")
        s_xt_hi = sem("graphs_t_high")
        s_xt_lo = sem("graphs_t_low")
        s_wt = sem("head_weights_transposed")
        s_wt_sb = sem("head_weights_t_in_sbuf")
        s_w_hi = sem("head_weights_high")
        s_w_lo = sem("head_weights_low")
        s_gram = sem("gram_done")
        s_gram_hi = sem("gram_high")
        s_gram_lo = sem("gram_low")

        a_sc = sem("scores_done")
        a_u = sem("scores_weighted")
        a_msk = sem("mask_done")
        a_nv = sem("masked_max_done")
        a_dd = sem("shifted_scores")
        a_st = sem("shifted_transposed")
        a_pt = sem("exp_done")
        a_av = sem("applied")
        a_rs = sem("reciprocal")
        a_pz = sem("normalised")
        h_y = sem("head_y_done")
        h_y_hi = sem("head_y_high")
        h_y_lo = sem("head_y_low")
        h_pz_hi = sem("head_normalised_high")
        h_pz_lo = sem("head_normalised_low")
        h_zt = sem("head_normalised_transposed")
        h_zt_sb = sem("head_normalised_t_in_sbuf")
        h_ct = sem("head_projected")
        h_cat = sem("head_projected_with_bias")
        h_lk = sem("head_leaky")
        h_cat_hi = sem("head_leaky_high")
        h_cat_lo = sem("head_leaky_low")
        h_wo = sem("head_projected_out")
        m_read = sem("mix_projection_read_out")
        m_ht_sb = sem("mix_ht_in_sbuf")
        m_tr = sem("mix_values_transposed")
        m_hv_sb = sem("mix_values_in_sbuf")
        m_bias = sem("mix_output_with_bias")
        m_lk = sem("mix_output_leaky")
        m_y = sem("mix_output_ready")
        s_out = sem("outputs_stored")
        s_apart = sem("apart")

        MIX_AT = SLOTS.index(MIX)

        class Slot:

            def __init__(self, r, at):
                self.kind, self.at = SLOTS[at], at
                self.is_mix = self.kind == MIX
                self.g = r - 1 if self.is_mix else r
                self.n = r * len(SLOTS) + at
                if type(r) is int and r == 0 and at < MIX_AT:
                    self.n = at + 1
                if type(r) is int and r == B:
                    self.n = r * len(SLOTS)
                self.r = r
                self.exists = type(self.g) is not int or 0 <= self.g < B
                self.mixes = self.g + 1
                if not self.is_mix:
                    self.heads = self.g * HEADS + (self.kind + 1)

            def at_or_later(self, n):
                return type(self.g) is not int or self.n >= n

            def after(self, heads):
                return type(self.g) is not int or self.heads > heads

            def head_before(self, k):
                at = self.at
                while k:
                    at -= 1
                    if SLOTS[at] != MIX:
                        k -= 1
                return slot_at(self.r, at)

        def slot_at(b, at):
            while at < 0:
                at += len(SLOTS)
                b = b - 1
            return Slot(b, at)

        def at_stage(b, p, stage):
            s = slot_at(b, p - LAG[stage])
            return s if s.exists else None

        def head_at(b, p, stage):
            s = at_stage(b, p, stage)
            return None if s is None or s.is_mix else s

        def mix_at(b, p, stage):
            s = at_stage(b, p, stage)
            return s if s is not None and s.is_mix else None

        def last_in_tile(b, p, stage):
            for back in (3, 6):
                s = slot_at(b, p - LAG[stage] - back)
                if s.exists:
                    return s

        def rounds(engine, body):
            body(0)
            body(1)
            with nc.Fori(2, B, engines=[engine]) as b:
                body(b)
            body(B)
            body(B + 1)

        def apart(eng):
            eng.sem_inc(s_apart, 1)

        block = ctx.enter_context(nc.Block())

        @block.sync
        def _(sp):
            xv = x.rearrange("b (p t) k -> p b (t k)", t=T)
            xd = xs[:, :, :, :].rearrange("p b t k -> p b (t k)")
            sp.dma_start(adj_raw[:, :, :], adj.rearrange("(p t) m -> p t m", t=T)).then_inc(s_ld_adj, 16)
            for c in range(CHUNKS):
                sp.dma_start(xd[:, c * CB:(c + 1) * CB, :], xv[:, c * CB:(c + 1) * CB, :]).then_inc(s_ld_x[c], 16)
            ov = out.rearrange("b (p t) k -> p b (t k)", t=T)

            def store(g):
                sp.wait_ge(m_y, g + 1)
                sp.dma_start(ov[:, bass.ds(g, 1), :], xd[:, bass.ds(g, 1), :]).then_inc(s_out, 16)

            with nc.Fori(0, B, engines=[mybir.EngineType.SP]) as g:
                store(g)
            sp.wait_ge(s_out, 16 * B)

        @block.gpsimd
        def _(pool):
            lw = l0_w.rearrange("(m k) o -> k m o", k=K)
            for r in range(2):
                pool.dma_start(l0_raw[r * K:(r + 1) * K, :, :], lw).then_inc(s_ld_w, 16)
            pool.dma_start(l0_bias[:, :], l0_b.partition_broadcast(P)).then_inc(s_ld_w, 16)
            for r in range(2):
                pool.dma_start(head_w[r * K:(r + 1) * K, :, :], wh.rearrange("h k d -> k h d")).then_inc(s_ld_w, 16)
            pool.dma_start(head_b_rows[:, :], bh).then_inc(s_ld_w, 16)
            pool.dma_start(out_w[:, :, :], w_out.rearrange("(h d) o -> d h o", d=D)).then_inc(s_ld_w, 16)
            pool.dma_start(out_b[:, :], b_out.partition_broadcast(P)).then_inc(s_ld_w, 16)
            pool.memset(ident[:, :], 0.0).then_inc(s_ident0, 1)
            pool.memset(conv_w[:, :, :], 0.0).then_inc(s_const, 1)
            pool.memset(eps[:, :], EPS).then_inc(s_const, 1)
            pool.memset(z[:, :, :, K:K + 1], 1.0).then_inc(s_const, 1)
            pool.memset(m_hv[:, :, K:K + 1], 1.0).then_inc(s_const, 1)
            pool.wait_ge(s_ident0, 1)
            pool.affine_select(out=ident[:, :], in_=ident[:, :], compare_op=ALU.not_equal, fill=1.0,
                               base=0, pattern=[[-1, P]], channel_multiplier=1).then_inc(s_const, 1)
            pool.wait_ge(s_ld_w, 8 * 16)
            for c in range(CHUNKS):
                pool.wait_ge(s_ld_x[c], 16)
                if c >= 2:
                    pool.wait_ge(s_x1, T * (c - 1))
                pool.tensor_tensor(xb[:, c % 2, :, :, :].rearrange("p b t k -> p (b t) k"),
                                   xs[:, c * CB:(c + 1) * CB, :, :].rearrange("p b t k -> p (b t) k"),
                                   l0_bias[:, :].unsqueeze(1).broadcast_to([P, CB * T, K]),
                                   ALU.add).then_inc(s_xb, 1)

            def shift(b, p):
                s = at_stage(b, p, "shifted")
                if s is None:
                    return
                pool.wait_ge(a_nv, s.n)
                apart(pool)
                for t in range(T):
                    here = nv[:, s.at % 3, t, :]
                    last = pool.tensor_scalar(here, here, -1.0, nmax[:, s.at % 3, t:t + 1], ALU.mult, ALU.add)
                last.then_inc(a_dd, 1)

            def product_low(b, p):
                s = at_stage(b, p, "part_lo")
                if s is None:
                    return
                if s.is_mix:
                    pool.wait_ge(a_pz, s.n)
                    apart(pool)
                    pool.tensor_tensor(m_o[:, :, :], pz[:, s.at % 3, :, :],
                                       out_b[:, :].unsqueeze(1).broadcast_to([P, T, K]), ALU.add).then_inc(m_bias, 1)
                    return
                pool.wait_ge(h_pz_hi, s.heads)
                apart(pool)
                pool.tensor_tensor(pz_parts[:, s.kind % 2, :, 1, :], pz[:, s.at % 3, :, :],
                                   pz_parts[:, s.kind % 2, :, 0, :].bitcast(F32), ALU.subtract).then_inc(h_pz_lo, 1)

            def out_low(b, p):
                s = at_stage(b, p, "out_lo")
                if s is None:
                    return
                if s.is_mix:
                    pool.wait_ge(m_lk, s.mixes)
                    apart(pool)
                    here = xs[:, bass.ds(s.g, 1), :, :].rearrange("p b t k -> p (b t) k")
                    pool.tensor_tensor(here, m_l[:, :, :], here, ALU.add).then_inc(m_y, 1)
                    return
                pool.wait_ge(h_cat_hi, s.heads)
                if s.after(2):
                    pool.wait_ge(h_wo, s.heads - 2)
                apart(pool)
                pool.tensor_tensor(cat_lo[:, s.kind % 2, :], cat[:, s.kind % 2, :],
                                   cat_hi[:, s.kind % 2, :].bitcast(F32), ALU.subtract).then_inc(h_cat_lo, 1)

            def attend(b):
                for p in range(len(SLOTS)):
                    shift(b, p)
                    product_low(b, p)
                    out_low(b, p)

            rounds(mybir.EngineType.Pool, attend)

        @block.scalar
        def _(act):
            def ln_act(n):
                act.wait_ge(s_ln, 4 * n + 2)
                act.activation(sq[:, :, :, :], hn[:, n % 2, :, :, :], ACT.Square).then_inc(s_ln_sq, 1)
                act.wait_ge(s_ln, 4 * n + 3)
                act.activation(ln_std[:, :], ln_var[:, :], ACT.Sqrt, scale=1.0 / K, bias=eps[:, :]).then_inc(s_ln_std, 1)

            def adj_copy():
                act.wait_ge(s_adj_tp, 1)
                act.activation(adj_t[:, :, :].rearrange("p t n -> p (t n)"), bank[0][:, :], ACT.Copy).then_inc(s_adj_t, 1)

            def conv_act(c):
                for i in range(2):
                    act.wait_ge(s_pt, 2 * c + i + 1)
                    if c >= 1 and i == 0:
                        act.wait_ge(s_cm, 3 * T * c)
                    act.activation(pair_t[:, 2 * i:2 * i + 2, :].rearrange("p a n -> p (a n)"), bank[i][:, :],
                                   ACT.Copy).then_inc(s_pt_sb, 1)
                for t in range(T):
                    act.wait_ge(s_cm, 3 * T * c + t + 1)
                    act.activation(conv_c[:, t, :], bank[2 + t][:, :], ACT.Copy).then_inc(s_cm_sb, 1)
                for t in range(T):
                    act.wait_ge(s_cm, 3 * T * c + T + t + 1)
                    act.activation(conv_d[:, t, :], bank[4 + t][:, :], ACT.Copy).then_inc(s_cm_sb, 1)

            act.wait_ge(s_const, 5)
            adj_copy()
            ln_act(0)
            ln_act(1)
            for c in range(CHUNKS):
                conv_act(c)
                if c + 2 < CHUNKS:
                    ln_act(c + 2)
            act.activation(head_hi[:, :, :], head_w[:, :, :], ACT.Copy).then_inc(s_w_hi, 1)
            act.activation(out_parts[:, :, 0, :], out_w[:, :, :], ACT.Copy).then_inc(s_w_hi, 1)
            act.wait_ge(s_wt, 1)
            for r in range(2):
                act.activation(head_wt[:, :, r, :], bank[0][:, :].rearrange("d (h k) -> d h k", h=HEADS),
                               ACT.Copy).then_inc(s_wt_sb, 1)
            act.activation(head_b[:, :], bank[1][:, 0:HEADS], ACT.Copy).then_inc(s_wt_sb, 1)
            for i in range(2):
                act.wait_ge(s_gram, i + 1)
                act.activation(gram[:, 4 * i:4 * i + 4, :].rearrange("p h k -> p (h k)"), bank[2 + i][:, :],
                               ACT.Copy).then_inc(s_gram_hi, 1)

            def doubled(c):
                act.wait_ge(s_hn, CHUNKS + T * (c + 1))
                if c >= 2:
                    act.wait_ge(s_xt, PAIRS * (c - 1))
                zc = z[:, c * CB:(c + 1) * CB, :, 0:K].rearrange("p b t k -> p t b k")
                for r in range(2):
                    act.activation(z_two[c % 2][:, :, :, r, :], zc, ACT.Copy).then_inc(s_two, 1)

            ln_act(CHUNKS)
            ln_act(CHUNKS + 1)
            doubled(0)
            doubled(1)
            for i in range(B // 2):
                act.wait_ge(s_xt, i + 1)
                act.activation(zt_hi[:, 2 * i:2 * i + 2, :].rearrange("k b n -> k (b n)"), bank[i % 2][:, :],
                               ACT.Copy).then_inc(s_xt_hi, 1)
                if i % PAIRS == PAIRS - 1 and i // PAIRS + 2 < CHUNKS:
                    ln_act(CHUNKS + i // PAIRS + 2)
                    doubled(i // PAIRS + 2)

            def y_high(b, p):
                s = at_stage(b, p, "y_hi")
                if s is None:
                    return
                if s.is_mix:
                    act.wait_ge(h_wo, (s.g + 1) * HEADS)
                    for r in range(2):
                        last = act.activation(m_parts[:, r, :], WO[r * K:(r + 1) * K, 0:N], ACT.Copy)
                    last.then_inc(m_read, 1)
                    return
                act.wait_ge(h_y, s.heads)
                if s.after(2):
                    act.wait_ge(a_sc, s.head_before(2).n)
                act.activation(y[:, s.kind % 2, :], Y[:, 0:N], ACT.Copy).then_inc(h_y_hi, 1)

            def values(b, p):
                s = mix_at(b, p, "values")
                if s is not None:
                    act.wait_ge(m_tr, s.mixes)
                    act.activation(m_hv[:, :, 0:K], HV[:, 0:T * K].rearrange("p (t k) -> p t k", t=T),
                                   ACT.Copy).then_inc(m_hv_sb, 1)

            def exponentials(b, p):
                s = at_stage(b, p, "exp")
                if s is None:
                    return
                act.wait_ge(a_st, s.n)
                before = last_in_tile(b, p, "exp")
                if before is not None:
                    act.wait_ge(a_av, before.n)
                act.activation(pt[:, s.at % 3, :, :].rearrange("p t n -> p (t n)"), ST[:, :], ACT.Exp).then_inc(a_pt, 1)

            def normalise(b, p):
                s = at_stage(b, p, "normalised")
                if s is None:
                    return
                act.wait_ge(a_rs, s.n)
                before = last_in_tile(b, p, "normalised")
                if before is not None:
                    act.wait_ge(m_bias if before.is_mix else h_pz_lo, before.mixes if before.is_mix else before.heads)
                for t in range(T):
                    last = act.activation(pz[:, s.at % 3, t, :], AV[:, t * (K + 1):t * (K + 1) + K], ACT.Copy,
                                          scale=rs[:, s.at % 3, t:t + 1])
                last.then_inc(a_pz, 1)

            def product_high(b, p):
                s = head_at(b, p, "part_hi")
                if s is None:
                    return
                act.wait_ge(a_pz, s.n)
                if s.after(2):
                    act.wait_ge(h_zt, s.heads - 2)
                act.activation(pz_parts[:, s.kind % 2, :, 0, :], pz[:, s.at % 3, :, :], ACT.Copy).then_inc(h_pz_hi, 1)

            def back_to_sbuf(b, p):
                s = head_at(b, p, "back_sb")
                if s is None:
                    return
                act.wait_ge(h_zt, s.heads)
                if s.after(2):
                    act.wait_ge(h_ct, s.heads - 2)
                act.activation(pzt[:, s.kind % 2, :], ZT[:, 0:N], ACT.Copy).then_inc(h_zt_sb, 1)

            def add_bias(b, p):
                s = head_at(b, p, "biased")
                if s is None:
                    return
                act.wait_ge(h_ct, s.heads)
                if s.after(2):
                    act.wait_ge(h_lk, s.heads - 2)
                act.activation(cat_raw[:, s.kind % 2, :], CT[:, 0:N], ACT.Identity, bias=head_b[:, s.kind:s.kind + 1])\
                   .then_inc(h_cat, 1)

            def out_high(b, p):
                s = head_at(b, p, "out_hi")
                if s is None:
                    return
                act.wait_ge(h_lk, s.heads)
                if s.after(2):
                    act.wait_ge(h_wo, s.heads - 2)
                act.activation(cat_hi[:, s.kind % 2, :], cat[:, s.kind % 2, :], ACT.Copy).then_inc(h_cat_hi, 1)

            def attend(b):
                for p in range(len(SLOTS)):
                    back_to_sbuf(b, p)
                    values(b, p)
                    product_high(b, p)
                    y_high(b, p)
                    out_high(b, p)
                    normalise(b, p)
                    exponentials(b, p)
                    add_bias(b, p)

            rounds(mybir.EngineType.Activation, attend)

        @block.vector
        def _(dve):
            dve.wait_ge(s_ld_w, 8 * 16)
            dve.wait_ge(s_const, 5)
            dve.tensor_tensor(l0_sum[:, :], l0_raw[:, 2, :], l0_raw[:, 4, :], ALU.add).then_inc(s_w_mix, 1)
            dve.wait_ge(s_w_mix, 1)
            for r in range(2):
                q = slice(r * K, (r + 1) * K)
                dve.tensor_tensor(conv_w[q, 0, q], l0_raw[q, 0, :], l0_sum[q, :], ALU.subtract)
                dve.tensor_tensor(conv_w[q, 1, q], l0_raw[q, 1, :], l0_raw[q, 3, :], ALU.add)
                dve.tensor_scalar(conv_w[q, 2, q], l0_sum[q, :], 2.0, None, ALU.mult).then_inc(s_w_mix, 1)
            dve.wait_ge(s_ld_adj, 16)
            for t in range(T):
                last = dve.tensor_scalar(neg_adj[:, t, :].rearrange("p (s q) -> p s q", s=T),
                                         adj_raw[:, t, :].rearrange("p (q s) -> p s q", s=T), -1.0, None, ALU.mult)
            last.then_inc(s_negadj, 1)

            def layernorm(n, c):
                src = xs[:, c * CB:(c + 1) * CB, :, :].rearrange("p b t k -> p t b k")
                dst = hn[:, n % 2, :, :, :].rearrange("p t b k -> p (t b) k")
                sqv = sq[:, :, :, :].rearrange("p t b k -> p (t b) k")

                def wide(a):
                    return a[:, :].unsqueeze(2).broadcast_to([P, CB * T, K])

                dve.tensor_reduce(ln_sum[:, :].rearrange("p (t b) -> p t b", t=T), src, AX.X, ALU.add).then_inc(s_ln, 1)
                dve.wait_ge(s_ln, 4 * n + 1)
                dve.tensor_scalar(ln_mean[:, :], ln_sum[:, :], 1.0 / K, None, ALU.mult).then_inc(s_ln_m, 1)
                dve.wait_ge(s_ln_m, n + 1)
                dve.tensor_tensor(hn[:, n % 2, :, :, :], src,
                                  wide(ln_mean).rearrange("p (t b) k -> p t b k", t=T), ALU.subtract).then_inc(s_ln, 1)
                dve.wait_ge(s_ln_sq, n + 1)
                dve.tensor_reduce(ln_var[:, :], sqv, AX.X, ALU.add).then_inc(s_ln, 1)
                dve.wait_ge(s_ln_std, n + 1)
                dve.reciprocal(ln_rs[:, :], ln_std[:, :]).then_inc(s_ln, 1)
                dve.wait_ge(s_ln, 4 * n + 4)
                if n < CHUNKS:
                    dve.scalar_tensor_tensor(dst, dst, 0.0, wide(ln_rs), ALU.max, ALU.mult).then_inc(s_hn, 1)
                    return
                for t in range(T):
                    dve.scalar_tensor_tensor(z[:, c * CB:(c + 1) * CB, t, 0:K], hn[:, n % 2, t, :, :], 0.0,
                                             ln_rs[:, t * CB:(t + 1) * CB].unsqueeze(2).broadcast_to([P, CB, K]),
                                             ALU.max, ALU.mult).then_inc(s_hn, 1)

            def first_norm(c):
                dve.wait_ge(s_ld_x[c], 16)
                if c >= 2:
                    dve.wait_ge(s_pt, 2 * (c - 1))
                layernorm(c, c)

            first_norm(0)
            first_norm(1)
            for c in range(CHUNKS):
                for t in range(T):
                    dve.wait_ge(s_cm, 3 * T * c + 2 * T + t + 1)
                    dve.wait_ge(s_xb, c + 1)
                    dve.tensor_tensor(xs[:, c * CB:(c + 1) * CB, t, :],
                                      bank[6 + t][:, :].rearrange("p (b k) -> p b k", b=CB),
                                      xb[:, c % 2, :, t, :], ALU.add).then_inc(s_x1, 1)
                if c + 2 < CHUNKS:
                    first_norm(c + 2)
            dve.wait_ge(s_w_hi, 2)
            dve.tensor_tensor(head_lo[:, :, :], head_w[:, :, :], head_hi[:, :, :].bitcast(F32), ALU.subtract).then_inc(s_w_lo, 1)
            dve.tensor_tensor(out_parts[:, :, 1, :], out_w[:, :, :], out_parts[:, :, 0, :].bitcast(F32), ALU.subtract).then_inc(s_w_lo, 1)
            for i in range(2):
                dve.wait_ge(s_gram_hi, i + 1)
                part = gram[K:P, 4 * i:4 * i + 4, :].rearrange("p h k -> p (h k)")
                dve.tensor_tensor(part, bank[2 + i][K:P, :], part.bitcast(F32), ALU.subtract).then_inc(s_gram_lo, 1)

            def low_parts(c):
                for i in range(c * PAIRS, (c + 1) * PAIRS):
                    dve.wait_ge(s_xt_hi, i + 1)
                    dve.tensor_tensor(zt_lo[:, 2 * i:2 * i + 2, :].rearrange("k b n -> k (b n)"), bank[i % 2][:, :],
                                      zt_hi[:, 2 * i:2 * i + 2, :].bitcast(F32).rearrange("k b n -> k (b n)"),
                                      ALU.subtract).then_inc(s_xt_lo, 1)

            for c in range(CHUNKS):
                dve.wait_ge(s_x1, T * (c + 1))
                layernorm(CHUNKS + c, c)
                if c >= 1:
                    low_parts(c - 1)
            low_parts(CHUNKS - 1)

            def weigh(b, p):
                s = at_stage(b, p, "weighted")
                if s is not None:
                    dve.wait_ge(a_sc, s.n)
                    dve.tensor_tensor(u[:, s.at % 3, :, :].rearrange("p t n -> p (t n)"), SC[:, :],
                                      neg_adj[:, :, :].rearrange("p t n -> p (t n)"), ALU.mult).then_inc(a_u, 1)

            def mask(b, p):
                s = at_stage(b, p, "mask")
                if s is not None:
                    dve.wait_ge(a_u, s.n)
                    if s.at_or_later(2):
                        dve.wait_ge(a_nv, s.n - 1)
                    dve.tensor_scalar(msk[:, :, :].rearrange("p t n -> p (t n)"),
                                      u[:, s.at % 3, :, :].rearrange("p t n -> p (t n)"), 0.0, NEG_INF,
                                      ALU.is_equal, ALU.mult).then_inc(a_msk, 1)

            def masked(b, p):
                s = at_stage(b, p, "masked")
                if s is None:
                    return
                dve.wait_ge(a_msk, s.n)
                before = last_in_tile(b, p, "masked")
                if before is not None:
                    dve.wait_ge(a_st, before.n)
                apart(dve)
                for t in range(T):
                    last = dve.tensor_tensor_reduce(nv[:, s.at % 3, t, :], msk[:, t, :], u[:, s.at % 3, t, :], 1.0, 3e38,
                                                    ALU.add, ALU.min, nmax[:, s.at % 3, t:t + 1])
                last.then_inc(a_nv, 1)

            def y_low(b, p):
                s = at_stage(b, p, "y_lo")
                if s is None:
                    return
                if s.is_mix:
                    dve.wait_ge(m_read, s.mixes)
                    dve.tensor_tensor(m_ht[:, :], m_parts[:, 0, :], m_parts[:, 1, :], ALU.add).then_inc(m_ht_sb, 1)
                    return
                dve.wait_ge(h_y_hi, s.heads)
                low = y[K:P, s.kind % 2, :]
                dve.tensor_tensor(low, Y[K:P, 0:N], low.bitcast(F32), ALU.subtract).then_inc(h_y_lo, 1)

            def reciprocal(b, p):
                s = at_stage(b, p, "reciprocal")
                if s is None:
                    return
                dve.wait_ge(a_av, s.n)
                before = last_in_tile(b, p, "reciprocal")
                if before is not None:
                    dve.wait_ge(a_pz, before.n)
                dve.reciprocal(rs[:, s.at % 3, :], AV[:, K:T * (K + 1):K + 1]).then_inc(a_rs, 1)

            def leaky(b, p):
                s = at_stage(b, p, "leaky")
                if s is None:
                    return
                if s.is_mix:
                    dve.wait_ge(m_bias, s.mixes)
                    dve.scalar_tensor_tensor(m_l[:, :, :], m_o[:, :, :], SLOPE, m_o[:, :, :],
                                             ALU.mult, ALU.max).then_inc(m_lk, 1)
                    return
                dve.wait_ge(h_cat, s.heads)
                if s.after(2):
                    dve.wait_ge(h_cat_lo, s.heads - 2)
                dve.scalar_tensor_tensor(cat[:, s.kind % 2, :], cat_raw[:, s.kind % 2, :], SLOPE,
                                         cat_raw[:, s.kind % 2, :], ALU.mult, ALU.max).then_inc(h_lk, 1)

            def attend(b):
                for p in range(len(SLOTS)):
                    masked(b, p)
                    weigh(b, p)
                    leaky(b, p)
                    mask(b, p)
                    reciprocal(b, p)
                    y_low(b, p)

            rounds(mybir.EngineType.DVE, attend)

        @block.tensor
        def _(pe):
            pe.wait_ge(s_const, 5)
            pe.wait_ge(s_ld_adj, 16)
            for s in range(T):
                for t in range(T):
                    last = pe.transpose(bank[0][:, s * N + t * P:s * N + (t + 1) * P],
                                        adj_raw[:, t, s:N:T], ident[:, :])
            last.then_inc(s_adj_tp, 1)

            def conv(c):
                pe.wait_ge(s_hn, c + 1)
                for i in range(2):
                    if c == 0 and i == 0:
                        pe.wait_ge(s_adj_t, 1)
                    if c >= 1:
                        pe.wait_ge(s_pt_sb, 2 * (c - 1) + i + 1)
                    for a in range(2):
                        for t in range(T):
                            g = 2 * (2 * i + a)
                            last = pe.transpose(bank[i][:, a * N + t * P:a * N + (t + 1) * P],
                                                hn[:, c % 2, t, g:g + 2, :].rearrange("p b k -> p (b k)"), ident[:, :])
                    last.then_inc(s_pt, 1)
                for step, (source, w) in enumerate([(None, 2), (conv_c, 1), (conv_d, 0)]):
                    for t in range(T):
                        out_bank = bank[2 + 2 * step + t]
                        if step < 2 and c >= 1:
                            pe.wait_ge(s_cm_sb, 2 * T * (c - 1) + T * step + t + 1)
                        if step == 2 and c >= 1:
                            pe.wait_ge(s_x1, T * (c - 1) + t + 1)
                        if source is not None:
                            pe.wait_ge(s_cm_sb, 2 * T * c + T * step)
                            for m in range(T):
                                pe.matmul(out_bank[:, :], adj_t[:, m, t * P:(t + 1) * P], source[:, m, :],
                                          start=(m == 0), stop=False, skip_group_check=True)
                        for a in range(PAIRS):
                            if step == 0:
                                pe.wait_ge(s_pt_sb, 2 * c + a // 2 + 1)
                            if step == 0 and c == 0:
                                pe.wait_ge(s_w_mix, 3)
                            last = pe.matmul(out_bank[:, a * P:(a + 1) * P], pair_t[:, a, t * P:(t + 1) * P],
                                             conv_w[:, w, :], start=(source is None and a == 0),
                                             stop=(a == PAIRS - 1), skip_group_check=True)
                        last.then_inc(s_cm, 1)

            for c in range(CHUNKS):
                conv(c)
            pe.wait_ge(s_x1, T * CHUNKS)
            for h in range(HEADS):
                pe.transpose(bank[0][:, h * K:(h + 1) * K], head_w[0:K, h, :], ident[0:K, 0:K])
            pe.transpose(bank[1][:, 0:HEADS], head_b_rows[:, :], ident[0:HEADS, 0:HEADS]).then_inc(s_wt, 1)
            pe.wait_ge(s_wt_sb, 3)
            for i in range(2):
                for h in range(4 * i, 4 * i + 4):
                    two = head_wt[:, h, :, :].rearrange("d r k -> d (r k)")
                    last = pe.matmul(bank[2 + i][:, (h % 4) * P:(h % 4 + 1) * P], two, two, start=True, stop=True)
                last.then_inc(s_gram, 1)
            for i in range(B // 2):
                c = i // PAIRS
                pe.wait_ge(s_two, 2 * (c + 1))
                if i >= 2:
                    pe.wait_ge(s_xt_lo, i - 1)
                for a in range(2):
                    for t in range(T):
                        g = 2 * (i % PAIRS) + a
                        last = pe.transpose(bank[i % 2][:, a * N + t * P:a * N + (t + 1) * P],
                                            z_two[c % 2][:, t, g, :, :].rearrange("p r k -> p (r k)"), ident[:, :])
                last.then_inc(s_xt, 1)
            pe.wait_ge(s_xt_lo, B // 2)
            pe.wait_ge(s_gram_lo, 2)
            pe.wait_ge(s_w_lo, 2)
            pe.wait_ge(s_negadj, 1)

            def weights_y(b, p):
                s = head_at(b, p, "y")
                if s is None:
                    return
                if s.after(1):
                    pe.wait_ge(h_y_lo, s.heads - 1)
                for i, part in enumerate((zt_hi, zt_lo)):
                    last = pe.matmul(Y[:, 0:N], gram[:, s.kind, :], part[:, bass.ds(s.g, 1), :].rearrange("k b n -> k (b n)"),
                                     start=(i == 0), stop=(i == 1))
                last.then_inc(h_y, 1)

            def scores(b, p):
                s = at_stage(b, p, "scores")
                if s is None:
                    return
                pe.wait_ge(m_ht_sb if s.is_mix else h_y_lo, s.mixes if s.is_mix else s.heads)
                if s.at_or_later(2):
                    pe.wait_ge(a_u, s.n - 1)
                if s.is_mix:
                    apart(pe)
                    for t in range(T):
                        last = pe.matmul(SC[:, t * N:(t + 1) * N], m_ht[:, t * P:(t + 1) * P], m_ht[:, :],
                                         start=True, stop=True)
                    last.then_inc(a_sc, 1)
                    for t in range(T):
                        last = pe.transpose(HV[:, t * K:(t + 1) * K], m_ht[:, t * P:(t + 1) * P], ident[0:K, 0:K])
                    last.then_inc(m_tr, 1)
                    return
                for t in range(T):
                    for i, part in enumerate((zt_hi, zt_lo)):
                        last = pe.matmul(SC[:, t * N:(t + 1) * N], y[:, s.kind % 2, t * P:(t + 1) * P],
                                         part[:, bass.ds(s.g, 1), :].rearrange("k b n -> k (b n)"),
                                         start=(i == 0), stop=(i == 1))
                last.then_inc(a_sc, 1)

            def transpose(b, p):
                s = at_stage(b, p, "transposed")
                if s is None:
                    return
                pe.wait_ge(a_dd, s.n)
                if s.at_or_later(2):
                    pe.wait_ge(a_pt, s.n - 1)
                for col in range(T):
                    for t in range(T):
                        last = pe.transpose(ST[:, col * N + t * P:col * N + (t + 1) * P],
                                            nv[:, s.at % 3, t, col * P:(col + 1) * P], ident[:, :])
                last.then_inc(a_st, 1)

            def apply(b, p):
                s = at_stage(b, p, "applied")
                if s is None:
                    return
                pe.wait_ge(a_pt, s.n)
                if s.is_mix:
                    pe.wait_ge(m_hv_sb, s.mixes)
                if s.at_or_later(2):
                    pe.wait_ge(a_pz, s.n - 1)
                for t in range(T):
                    for m in range(T):
                        val = m_hv[:, m, :] if s.is_mix else z[:, bass.ds(s.g, 1), m, :].rearrange("p b k -> p (b k)")
                        last = pe.matmul(AV[:, t * (K + 1):(t + 1) * (K + 1)], pt[:, s.at % 3, m, t * P:(t + 1) * P],
                                         val, start=(m == 0), stop=(m == T - 1))
                last.then_inc(a_av, 1)

            def transpose_back(b, p):
                s = head_at(b, p, "back")
                if s is None:
                    return
                pe.wait_ge(h_pz_lo, s.heads)
                if s.after(1):
                    pe.wait_ge(h_zt_sb, s.heads - 1)
                for t in range(T):
                    last = pe.transpose(ZT[:, t * P:(t + 1) * P],
                                        pz_parts[:, s.kind % 2, t, :, :].bitcast(F32).rearrange("p r k -> p (r k)"),
                                        ident[:, :])
                last.then_inc(h_zt, 1)

            def project(b, p):
                s = head_at(b, p, "projected")
                if s is None:
                    return
                pe.wait_ge(h_zt_sb, s.heads)
                if s.after(1):
                    pe.wait_ge(h_cat, s.heads - 1)
                for i, part in enumerate((head_hi, head_lo)):
                    last = pe.matmul(CT[:, 0:N], part[:, s.kind, :], pzt[:, s.kind % 2, :], start=(i == 0), stop=(i == 1))
                last.then_inc(h_ct, 1)

            def project_out(b, p):
                s = head_at(b, p, "out")
                if s is None:
                    return
                pe.wait_ge(h_cat_lo, s.heads)
                if s.kind == 0 and s.after(1):
                    pe.wait_ge(m_read, s.g)
                two = out_parts[:, s.kind, :, :].rearrange("d r k -> d (r k)")
                for i, part in enumerate((cat_hi, cat_lo)):
                    last = pe.matmul(WO[:, 0:N], two, part[:, s.kind % 2, :], start=(s.kind == 0 and i == 0),
                                     stop=(s.kind == HEADS - 1 and i == 1), skip_group_check=True)
                last.then_inc(h_wo, 1)

            def attend(b):
                for p in range(len(SLOTS)):
                    weights_y(b, p)
                    apply(b, p)
                    project(b, p)
                    transpose(b, p)
                    transpose_back(b, p)
                    scores(b, p)
                    project_out(b, p)

            rounds(mybir.EngineType.PE, attend)


_INS = ["x", "adj", "L0_gnn_weight", "L0_gnn_bias", "L1_gnn_Wh", "L1_gnn_bh", "L1_gnn_W_out", "L1_gnn_b_out"]
_OUTS = [((32, 256, 64), "float32")]


def kernel(**inputs):
    import numpy as _np
    import concourse.bacc as _bacc
    from concourse import mybir as _mybir
    from concourse.bass_utils import run_bass_kernel_spmd as _run

    nc = _bacc.Bacc("TRN2", target_bir_lowering=False, num_devices=1)
    arrays, args = {}, []
    for name in _INS:
        a = _np.ascontiguousarray(inputs[name])
        arrays[f"in_{name}_dram"] = a
        args.append(nc.dram_tensor(f"in_{name}_dram", a.shape, _mybir.dt.from_np(a.dtype), kind="ExternalInput").ap())
    for i, (shape, dtype) in enumerate(_OUTS):
        dt = _mybir.dt.from_np(_np.dtype(dtype))
        args.append(nc.dram_tensor(f"out_{i}_dram", shape, dt, kind="ExternalOutput").ap())
    graph_block(nc, *args)
    r = _run(nc, [arrays], core_ids=[0])
    got = tuple(r.results[0][f"out_{i}_dram"] for i in range(len(_OUTS)))
    return got[0]
```

```python
import concourse.bass as bass
from concourse import mybir
from contextlib import ExitStack

P = 128
NEG_INF = 1e16
SLOPE = 0.01
EPS = 1e-5

MIX = "mix"
SLOTS = [0, 1, 2, 3, 4, 5, 6, 7, MIX]
LAG = dict(y=0, y_hi=0, read=-1, y_lo=0, scores=2, values=2, weighted=1, mask=1, masked=2, shifted=2,
           transposed=4, exp=3, applied=5, reciprocal=5, normalised=4, mix_bias=7, back=6, part_hi=6,
           part_lo=7, projected=8, biased=7, leaky=8, mix_leaky=9, residual=9, out=9)


def graph_block(nc, x, adj, l0_w, l0_b, wh, bh, w_out, b_out, out):
    F32 = mybir.dt.float32
    F32R = mybir.dt.float32r
    ALU = mybir.AluOpType
    ACT = mybir.ActivationFunctionType
    AX = mybir.AxisListType

    B, N, K = x.shape
    HEADS, _, D = wh.shape
    T = N // P
    NM = l0_w.shape[0] // K
    CB = 8
    CHUNKS = B // CB
    PAIRS = CB // 2
    BK = CB * K

    ctx = ExitStack()
    with ctx:
        def sb(name, shape, dt=F32):
            return ctx.enter_context(nc.sbuf_tensor(name, shape, dt))

        def sem(name):
            return ctx.enter_context(nc.semaphore(name))

        bank = [ctx.enter_context(nc.psum_tensor(f"bank{i}", [P, 512], F32)) for i in range(8)]

        ident = sb("ident", [P, P])
        adj_raw = sb("adj_raw", [P, T, N])
        neg_adj = sb("neg_adj", [P, T, N])
        adj_t = sb("adj_t", [P, T, N])
        l0_raw = sb("l0_raw", [P, NM, K])
        l0_sum = sb("l0_sum", [P, K])
        conv_w = sb("conv_w", [P, 3, P])
        l0_bias = sb("l0_bias", [P, K])
        head_w = sb("head_w", [P, HEADS, D])
        head_wt = sb("head_wt", [D, HEADS, 2, K])
        head_b_rows = sb("head_b_rows", [HEADS, D])
        head_b = sb("head_b", [D, 2, HEADS])
        head_hi = sb("head_hi", [P, HEADS, D], F32R)
        head_lo = sb("head_lo", [P, HEADS, D], F32R)
        gram = sb("gram", [P, HEADS, K], F32R)
        out_w = sb("out_w", [D, HEADS, 2, K])
        out_b = sb("out_b", [P, K])

        xs = sb("xs", [P, B, T, K])
        hn = sb("hn", [P, 3, T, CB, K])
        sq = sb("sq", [P, T, CB, K])
        ln_sum = sb("ln_sum", [P, 2, CB * T])
        ln_mean = sb("ln_mean", [P, 2, CB * T])
        ln_var = sb("ln_var", [P, 2, CB * T])
        ln_eps = sb("ln_eps", [P, 2, CB * T])
        ln_rs = sb("ln_rs", [P, 2, CB * T])
        minus_half = sb("minus_half", [P, CB * T])
        pair_t = sb("pair_t", [P, 2, PAIRS, N])
        conv_cd = sb("conv_cd", [P, 2, T, BK])
        conv_c, conv_d = conv_cd[:, 0, :, :], conv_cd[:, 1, :, :]
        scratch = sb("scratch", [P, 2 * T * CB * 2 * K])
        z_two = scratch[:, :].rearrange("p (c t b r k) -> p c t b r k", c=2, t=T, b=CB, r=2)
        z_last = conv_cd[:, :, :, :].rearrange("p a t (b k) -> p (a t b k)", k=K)\
            .rearrange("p (t b r k) -> p t b r k", t=T, b=CB, r=2)
        z = sb("z", [P, B, T, K + 1])
        zt_hi = sb("zt_hi", [P, B, N], F32R)
        zt_lo = sb("zt_lo", [P, B, N], F32R)

        u = sb("u", [P, 3, T, N])
        msk = scratch[:, 6 * T * N:7 * T * N].rearrange("p (t n) -> p t n", t=T)
        nv = scratch[:, 0:3 * T * N].rearrange("p (i t n) -> p i t n", i=3, t=T)
        nmax = sb("nmax", [P, 3, T])
        pt = scratch[:, 3 * T * N:6 * T * N].rearrange("p (i t n) -> p i t n", i=3, t=T)
        rs = sb("rs", [P, 3, T])
        pz = sb("pz", [P, 2, T, 2, K])
        y = sb("y", [P, 2, N], F32R)
        pzt = sb("pzt", [P, 2, N], F32R)
        cat_raw = sb("cat_raw", [D, 2, 2, N])
        cat = sb("cat", [D, 2, N])
        m_ht = sb("m_ht", [P, N])
        m_hi = sb("m_hi", [P, N], F32R)
        m_lo = sb("m_lo", [P, N], F32R)
        m_stack = sb("m_stack", [P, N], F32R)
        m_hv = sb("m_hv", [P, T, K + 1])
        m_pz = sb("m_pz", [P, T, K])
        m_o = sb("m_o", [P, T, K])
        m_l = sb("m_l", [P, T, K])

        Y, HV, SC, ST, AV, CT, WO, ZT = bank
        XT = [bank[0], bank[1], bank[6], bank[7]]

        def xt_bank(c, j):
            return HV if c == CHUNKS - 1 else XT[j]

        s_ld_x = [sem(f"x_loaded{c}") for c in range(CHUNKS)]
        s_ld_adj = sem("adj_loaded")
        s_ld_l0 = sem("conv_weights_loaded")
        s_ld_w = sem("weights_loaded")
        s_ident0 = sem("ident_zeroed")
        s_const = sem("constants_ready")
        s_w_mix = sem("conv_weights_steps")
        s_negadj = sem("neg_adj_ready")
        s_adj_tp = sem("adj_transposed")
        s_adj_t = sem("adj_t_in_sbuf")
        s_ln_sum = sem("layernorm_sum")
        s_ln_m = sem("layernorm_mean")
        s_ln_sub = sem("layernorm_centred")
        s_ln_sq = sem("layernorm_squares")
        s_ln_var = sem("layernorm_variance")
        s_ln_eps = sem("layernorm_variance_guarded")
        s_ln_rs = sem("layernorm_reciprocal_deviation")
        s_hn = sem("first_layernorm_ready")
        s_z = sem("second_layernorm_ready")
        s_xb = sem("residual_with_bias")
        s_pt = sem("pairs_transposed")
        s_pt_sb = sem("pairs_in_sbuf")
        s_c0 = sem("conv_first_product")
        s_c1 = sem("conv_second_product")
        s_c2 = sem("conv_third_product")
        s_cc = sem("conv_first_in_sbuf")
        s_cd = sem("conv_second_in_sbuf")
        s_x1 = sem("x1_ready")
        s_two = sem("layernorm_doubled")
        s_xt = sem("graphs_transposed")
        s_xt_hi = sem("graphs_t_high")
        s_xt_lo = sem("graphs_t_low")
        s_wt = sem("head_weights_transposed")
        s_wt_sb = sem("head_weights_t_in_sbuf")
        s_w_hi = sem("head_weights_high")
        s_w_lo = sem("head_weights_low")
        s_gram = sem("gram_done")
        s_gram_hi = sem("gram_high")
        s_gram_lo = sem("gram_low")

        a_sc = sem("scores_done")
        a_u = sem("scores_weighted")
        a_msk = sem("mask_done")
        a_nv = sem("masked_max_done")
        a_dd = sem("shifted_scores")
        a_st = sem("shifted_transposed")
        a_pt = sem("exp_done")
        a_av = sem("applied")
        a_rs = sem("reciprocal")
        a_pz = sem("normalised")
        p_y = sem("pair_y_done")
        p_zt = sem("pair_normalised_transposed")
        h_y_hi = sem("head_y_high")
        h_y_lo = sem("head_y_low")
        h_pzt_hi = sem("head_normalised_t_high")
        h_pzt_lo = sem("head_normalised_t_low")
        h_ct = sem("head_projected")
        h_cat = sem("head_projected_with_bias")
        h_lk = sem("head_leaky")
        h_wo = sem("head_projected_out")
        m_ht_sb = sem("mix_ht_in_sbuf")
        m_ht_hi = sem("mix_ht_high")
        m_ht_lo = sem("mix_ht_low")
        m_tr = sem("mix_values_transposed")
        m_hv_sb = sem("mix_values_in_sbuf")
        m_bias = sem("mix_output_with_bias")
        m_lk = sem("mix_output_leaky")
        m_y = sem("mix_output_ready")
        s_out = sem("outputs_stored")
        s_apart = sem("apart")

        MIX_AT = SLOTS.index(MIX)

        class Slot:

            def __init__(self, r, at):
                self.kind, self.at = SLOTS[at], at
                self.is_mix = self.kind == MIX
                self.g = r - 1 if self.is_mix else r
                self.n = r * len(SLOTS) + at
                if type(r) is int and r == 0 and at < MIX_AT:
                    self.n = at + 1
                if type(r) is int and r == B:
                    self.n = r * len(SLOTS)
                self.r = r
                self.exists = type(self.g) is not int or 0 <= self.g < B
                self.mixes = self.g + 1
                if not self.is_mix:
                    self.heads = self.g * HEADS + (self.kind + 1)
                    self.pairs = self.g * (HEADS // 2) + (self.kind // 2 + 1)
                    self.half = self.kind // 2 % 2
                    self.odd = self.kind % 2
                    self.rows = slice(self.odd * K, (self.odd + 1) * K)
                    self.other_rows = slice((1 - self.odd) * K, (2 - self.odd) * K)

            def at_or_later(self, n):
                return type(self.g) is not int or self.n >= n

            def after(self, heads):
                return type(self.g) is not int or self.heads > heads

            def head_before(self, k):
                at = self.at
                while k:
                    at -= 1
                    if SLOTS[at] != MIX:
                        k -= 1
                return slot_at(self.r, at)

        def slot_at(b, at):
            while at < 0:
                at += len(SLOTS)
                b = b - 1
            while at >= len(SLOTS):
                at -= len(SLOTS)
                b = b + 1
            return Slot(b, at)

        def at_stage(b, p, stage):
            s = slot_at(b, p - LAG[stage])
            return s if s.exists else None

        def head_at(b, p, stage):
            s = at_stage(b, p, stage)
            return None if s is None or s.is_mix else s

        def mix_at(b, p, stage):
            s = at_stage(b, p, stage)
            return s if s is not None and s.is_mix else None

        def last_in_tile(b, p, stage):
            for back in (3, 6):
                s = slot_at(b, p - LAG[stage] - back)
                if s.exists:
                    return s

        def rounds(engine, body):
            body(0)
            body(1)
            with nc.Fori(2, B, engines=[engine]) as b:
                body(b)
            body(B)
            body(B + 1)

        LATE = dict(centre=1, squares=2, variance=3, power=4, norm=5, doubled=5, transposed=[8, 11, 14, 17],
                    high=[7, 10, 13, 16], low=[8, 11, 14, 17])
        LAST = CHUNKS - 1

        def late_slot(b, p):
            return b * len(SLOTS) + p if type(b) is int and b < 2 else None

        def apart(eng):
            eng.sem_inc(s_apart, 1)

        def norm_number(which, c):
            order = [(1, 0), (1, 1), (1, 2)]
            for k in range(CHUNKS):
                order.append((2, k))
                if k + 3 < CHUNKS:
                    order.append((1, k + 3))
            return order.index((which, c))

        block = ctx.enter_context(nc.Block())

        @block.sync
        def _(sp):
            xv = x.rearrange("b (p t) k -> p b (t k)", t=T)
            xd = xs[:, :, :, :].rearrange("p b t k -> p b (t k)")
            for c in range(CHUNKS):
                sp.dma_start(xd[:, c * CB:(c + 1) * CB, :], xv[:, c * CB:(c + 1) * CB, :]).then_inc(s_ld_x[c], 16)
                if c == 0:
                    sp.dma_start(adj_raw[:, :, :], adj.rearrange("(p t) m -> p t m", t=T)).then_inc(s_ld_adj, 16)
            ov = out.rearrange("b (p t) k -> p b (t k)", t=T)

            def store(g):
                sp.wait_ge(m_y, g + 1)
                sp.dma_start(ov[:, bass.ds(g, 1), :], xd[:, bass.ds(g, 1), :]).then_inc(s_out, 16)

            with nc.Fori(0, B, engines=[mybir.EngineType.SP]) as g:
                store(g)
            sp.wait_ge(s_out, 16 * B)

        @block.gpsimd
        def _(pool):
            pool.memset(ident[:, :], 0.0).then_inc(s_ident0, 1)
            pool.memset(minus_half[:, :], -0.5).then_inc(s_const, 1)
            pool.memset(conv_w[:, :, :], 0.0).then_inc(s_const, 1)
            pool.memset(z[:, :, :, K:K + 1], 1.0).then_inc(s_const, 1)
            pool.memset(m_hv[:, :, K:K + 1], 1.0).then_inc(s_const, 1)
            pool.wait_ge(s_ident0, 1)
            pool.affine_select(out=ident[:, :], in_=ident[:, :], compare_op=ALU.not_equal, fill=1.0,
                               base=0, pattern=[[-1, P]], channel_multiplier=1).then_inc(s_const, 1)
            def squares(which, c):
                n = norm_number(which, c)
                pool.wait_ge(s_ln_sub, n + 1)
                if n >= 1:
                    pool.wait_ge(s_ln_var, n)
                here = hn[:, 2 if which == 2 else c % 2, :, :, :].rearrange("p t b k -> p (t b k)")
                pool.tensor_tensor(sq[:, :, :, :].rearrange("p t b k -> p (t b k)"), here, here, ALU.mult)\
                    .then_inc(s_ln_sq, 1)

            def power(which, c):
                pool.wait_ge(s_ln_eps, norm_number(which, c) + 1)
                pool.tensor_tensor(ln_rs[:, which - 1, :], ln_eps[:, which - 1, :], minus_half[:, :], ALU.pow)\
                    .then_inc(s_ln_rs, 1)

            def residual_bias(c):
                pool.wait_ge(s_ln_sub, norm_number(1, c) + 1)
                if c == 0:
                    pool.wait_ge(s_ld_l0, 3 * 16)
                here = xs[:, c * CB:(c + 1) * CB, :, :].rearrange("p b t k -> p (b t) k")
                pool.tensor_tensor(here, here, l0_bias[:, :].unsqueeze(1).broadcast_to([P, CB * T, K]),
                                   ALU.add).then_inc(s_xb, 1)

            pool.wait_ge(s_const, 5)
            for c in range(2):
                squares(1, c)
                power(1, c)
                residual_bias(c)
            squares(1, 2)
            for c in range(CHUNKS):
                if c + 2 < CHUNKS:
                    power(1, c + 2)
                    residual_bias(c + 2)
                if c != LAST:
                    squares(2, c)
                    power(2, c)
                if c + 3 < CHUNKS:
                    squares(1, c + 3)

            def late(b, p):
                if late_slot(b, p) == LATE["squares"]:
                    squares(2, LAST)
                if late_slot(b, p) == LATE["power"]:
                    power(2, LAST)

            def shift(b, p):
                s = at_stage(b, p, "shifted")
                if s is None:
                    return
                pool.wait_ge(a_nv, s.n)
                apart(pool)
                for t in range(T):
                    here = nv[:, s.at % 3, t, :]
                    last = pool.tensor_scalar(here, here, -1.0, nmax[:, s.at % 3, t:t + 1], ALU.mult, ALU.add)
                last.then_inc(a_dd, 1)

            def mix_bias(b, p):
                s = mix_at(b, p, "mix_bias")
                if s is not None:
                    pool.wait_ge(a_pz, s.n)
                    apart(pool)
                    pool.tensor_tensor(m_o[:, :, :], m_pz[:, :, :], out_b[:, :].unsqueeze(1).broadcast_to([P, T, K]),
                                       ALU.add).then_inc(m_bias, 1)

            def leaky(b, p):
                s = head_at(b, p, "leaky")
                if s is None:
                    return
                pool.wait_ge(h_cat, s.heads)
                if s.after(2):
                    pool.wait_ge(h_wo, s.heads - 2)
                apart(pool)
                pool.tensor_tensor(cat[:, s.odd, :], cat_raw[:, s.odd, 0, :], cat_raw[:, s.odd, 1, :],
                                   ALU.subtract).then_inc(h_lk, 1)

            def residual(b, p):
                s = mix_at(b, p, "residual")
                if s is not None:
                    pool.wait_ge(m_lk, s.mixes)
                    apart(pool)
                    here = xs[:, bass.ds(s.g, 1), :, :].rearrange("p b t k -> p (b t) k")
                    pool.tensor_tensor(here, m_l[:, :, :], here, ALU.add).then_inc(m_y, 1)

            def attend(b):
                for p in range(len(SLOTS)):
                    leaky(b, p)
                    mix_bias(b, p)
                    shift(b, p)
                    residual(b, p)
                    late(b, p)

            rounds(mybir.EngineType.Pool, attend)

        @block.scalar
        def _(act):
            def pairs_to_sbuf(c):
                for i in range(2):
                    act.wait_ge(s_pt, 2 * c + i + 1)
                    if c >= 2 and i == 0:
                        act.wait_ge(s_c2, T * (c - 1))
                    act.activation(pair_t[:, c % 2, 2 * i:2 * i + 2, :].rearrange("p a n -> p (a n)"), bank[i][:, :],
                                   ACT.Copy).then_inc(s_pt_sb, 1)

            def first_to_sbuf(c):
                for t in range(T):
                    act.wait_ge(s_c0, T * c + t + 1)
                    if c >= 1 and t == 0:
                        act.wait_ge(s_c1, T * c)
                    act.activation(conv_c[:, t, :], bank[2 + t][:, :], ACT.Copy).then_inc(s_cc, 1)

            def second_to_sbuf(c):
                for t in range(T):
                    act.wait_ge(s_c1, T * c + t + 1)
                    if c >= 1 and t == 0:
                        act.wait_ge(s_c2, T * c)
                    act.activation(conv_d[:, t, :], bank[4 + t][:, :], ACT.Copy).then_inc(s_cd, 1)

            def doubled(c):
                act.wait_ge(s_z, T * (c + 1))
                if c >= 2:
                    act.wait_ge(s_xt, PAIRS * (c - 1))
                zc = z[:, c * CB:(c + 1) * CB, :, 0:K].rearrange("p b t k -> p t b k")
                for r in range(2):
                    to = z_last if c == LAST else z_two[:, c % 2]
                    act.activation(to[:, :, :, r, :], zc, ACT.Copy).then_inc(s_two, 1)

            def graphs_high(c, pairs):
                for j in pairs:
                    i = c * PAIRS + j
                    act.wait_ge(s_xt, i + 1)
                    act.activation(zt_hi[:, 2 * i:2 * i + 2, :].rearrange("k b n -> k (b n)"), xt_bank(c, j)[:, :],
                                   ACT.Copy).then_inc(s_xt_hi, 1)

            lw = l0_w.rearrange("(m k) o -> k m o", k=K)
            for r in range(2):
                act.dma_start(l0_raw[r * K:(r + 1) * K, :, :], lw).then_inc(s_ld_l0, 16)
            act.dma_start(l0_bias[:, :], l0_b.partition_broadcast(P)).then_inc(s_ld_l0, 16)
            for r in range(2):
                act.dma_start(head_w[r * K:(r + 1) * K, :, :], wh.rearrange("h k d -> k h d")).then_inc(s_ld_w, 16)
            act.dma_start(head_b_rows[:, :], bh).then_inc(s_ld_w, 16)
            for r in range(2):
                act.dma_start(out_w[:, :, r, :], w_out.rearrange("(h d) o -> d h o", d=D)).then_inc(s_ld_w, 16)
            act.dma_start(out_b[:, :], b_out.partition_broadcast(P)).then_inc(s_ld_w, 16)
            act.wait_ge(s_const, 5)
            act.wait_ge(s_adj_tp, 1)
            act.activation(adj_t[:, :, :].rearrange("p t n -> p (t n)"), bank[0][:, :], ACT.Copy).then_inc(s_adj_t, 1)
            pairs_to_sbuf(0)
            first_to_sbuf(0)
            for c in range(CHUNKS):
                second_to_sbuf(c)
                if c == LAST:
                    act.wait_ge(s_ld_w, 6 * 16)
                    act.wait_ge(s_wt, 1)
                    for r in range(2):
                        act.activation(head_wt[:, :, r, :], bank[2][:, :].rearrange("d (h k) -> d h k", h=HEADS),
                                       ACT.Copy).then_inc(s_wt_sb, 1)
                    act.activation(head_b[:, 0, :], bank[3][:, 0:HEADS], ACT.Copy)
                    act.activation(head_b[:, 1, :], bank[3][:, 0:HEADS], ACT.Copy, scale=-SLOPE).then_inc(s_wt_sb, 1)
                    act.activation(head_hi[:, :, :], head_w[:, :, :], ACT.Copy).then_inc(s_w_hi, 1)
                if c + 1 < CHUNKS:
                    pairs_to_sbuf(c + 1)
                    first_to_sbuf(c + 1)
                if c >= 1:
                    doubled(c - 1)
                    graphs_high(c - 1, range(PAIRS))
            act.wait_ge(s_gram, 1)
            act.activation(gram[:, :, :].rearrange("p h k -> p (h k)"), bank[3][:, :], ACT.Copy).then_inc(s_gram_hi, 1)

            def late(b, p):
                if late_slot(b, p) == LATE["doubled"]:
                    doubled(LAST)
                if late_slot(b, p) in LATE["high"]:
                    graphs_high(LAST, [LATE["high"].index(late_slot(b, p))])

            def read(b, p):
                s = mix_at(b, p, "read")
                if s is not None:
                    act.wait_ge(h_wo, (s.g + 1) * HEADS)
                    act.activation(m_ht[:, :], WO[:, 0:N], ACT.Copy).then_inc(m_ht_sb, 1)

            def y_high(b, p):
                s = at_stage(b, p, "y_hi")
                if s is None:
                    return
                if s.is_mix:
                    act.wait_ge(m_ht_sb, s.mixes)
                    act.activation(m_hi[:, :], m_ht[:, :], ACT.Copy)
                    act.activation(m_stack[0:K, :], m_ht[0:K, :], ACT.Copy).then_inc(m_ht_hi, 1)
                    return
                act.wait_ge(p_y, s.pairs)
                if s.after(2):
                    act.wait_ge(a_sc, s.head_before(2).n)
                act.activation(y[s.rows, s.odd, :], Y[s.rows, 0:N], ACT.Copy).then_inc(h_y_hi, 1)

            def values(b, p):
                s = mix_at(b, p, "values")
                if s is not None:
                    act.wait_ge(m_tr, s.mixes)
                    act.activation(m_hv[:, :, 0:K], HV[:, 0:T * K].rearrange("p (t k) -> p t k", t=T),
                                   ACT.Copy).then_inc(m_hv_sb, 1)

            def exponentials(b, p):
                s = at_stage(b, p, "exp")
                if s is None:
                    return
                act.wait_ge(a_st, s.n)
                before = last_in_tile(b, p, "exp")
                if before is not None:
                    act.wait_ge(a_av, before.n)
                act.activation(pt[:, s.at % 3, :, :].rearrange("p t n -> p (t n)"), ST[:, :], ACT.Exp).then_inc(a_pt, 1)

            def normalise(b, p):
                s = at_stage(b, p, "normalised")
                if s is None:
                    return
                act.wait_ge(a_rs, s.n)
                if not s.is_mix and s.after(4):
                    act.wait_ge(p_zt, s.pairs - 2)
                for t in range(T):
                    here = m_pz[:, t, :] if s.is_mix else pz[:, s.half, t, s.odd, :]
                    last = act.activation(here, AV[:, t * (K + 1):t * (K + 1) + K], ACT.Copy,
                                          scale=rs[:, s.at % 3, t:t + 1])
                last.then_inc(a_pz, 1)

            def product_high(b, p):
                s = head_at(b, p, "part_hi")
                if s is None:
                    return
                act.wait_ge(p_zt, s.pairs)
                if s.after(2):
                    act.wait_ge(h_ct, s.heads - 2)
                act.activation(pzt[s.rows, s.odd, :], ZT[s.rows, 0:N], ACT.Copy).then_inc(h_pzt_hi, 1)

            def add_bias(b, p):
                s = head_at(b, p, "biased")
                if s is None:
                    return
                act.wait_ge(h_ct, s.heads)
                if s.after(2):
                    act.wait_ge(h_lk, s.heads - 2)
                source = CT[:, 0:N]
                act.activation(cat_raw[:, s.odd, 0, :], source, ACT.Relu, bias=head_b[:, 0, s.kind:s.kind + 1])
                act.activation(cat_raw[:, s.odd, 1, :], source, ACT.Relu, bias=head_b[:, 1, s.kind:s.kind + 1],
                               scale=-SLOPE).then_inc(h_cat, 1)

            def attend(b):
                for p in range(len(SLOTS)):
                    y_high(b, p)
                    product_high(b, p)
                    values(b, p)
                    read(b, p)
                    exponentials(b, p)
                    add_bias(b, p)
                    normalise(b, p)
                    late(b, p)

            rounds(mybir.EngineType.Activation, attend)

        @block.vector
        def _(dve):
            def centre(which, c):
                n = norm_number(which, c)
                w = which - 1
                of = 2 if which == 2 else c % 2
                if which == 1:
                    dve.wait_ge(s_ld_x[c], 16)
                    if c >= 2:
                        dve.wait_ge(s_pt, 2 * (c - 1))
                src = xs[:, c * CB:(c + 1) * CB, :, :].rearrange("p b t k -> p t b k")
                dve.tensor_reduce(ln_sum[:, w, :].rearrange("p (t b) -> p t b", t=T), src, AX.X, ALU.add)\
                   .then_inc(s_ln_sum, 1)
                dve.wait_ge(s_ln_sum, n + 1)
                dve.tensor_scalar(ln_mean[:, w, :], ln_sum[:, w, :], 1.0 / K, None, ALU.mult).then_inc(s_ln_m, 1)
                dve.wait_ge(s_ln_m, n + 1)
                dve.tensor_tensor(hn[:, of, :, :, :], src,
                                  ln_mean[:, w, :].unsqueeze(2).broadcast_to([P, CB * T, K])
                                  .rearrange("p (t b) k -> p t b k", t=T), ALU.subtract).then_inc(s_ln_sub, 1)

            def variance(which, c):
                n = norm_number(which, c)
                w = which - 1
                dve.wait_ge(s_ln_sq, n + 1)
                dve.tensor_reduce(ln_var[:, w, :], sq[:, :, :, :].rearrange("p t b k -> p (t b) k"), AX.X, ALU.add)\
                   .then_inc(s_ln_var, 1)
                dve.wait_ge(s_ln_var, n + 1)
                dve.tensor_scalar(ln_eps[:, w, :], ln_var[:, w, :], 1.0 / K, EPS, ALU.mult, ALU.add).then_inc(s_ln_eps, 1)

            def first_norm(c):
                dve.wait_ge(s_ln_rs, norm_number(1, c) + 1)
                here = hn[:, c % 2, :, :, :].rearrange("p t b k -> p (t b) k")
                dve.scalar_tensor_tensor(here, here, 0.0, ln_rs[:, 0, :].unsqueeze(2).broadcast_to([P, CB * T, K]),
                                         ALU.max, ALU.mult).then_inc(s_hn, 1)

            def second_norm(c):
                dve.wait_ge(s_ln_rs, norm_number(2, c) + 1)
                for t in range(T):
                    dve.scalar_tensor_tensor(z[:, c * CB:(c + 1) * CB, t, 0:K], hn[:, 2, t, :, :], 0.0,
                                             ln_rs[:, 1, t * CB:(t + 1) * CB].unsqueeze(2).broadcast_to([P, CB, K]),
                                             ALU.max, ALU.mult).then_inc(s_z, 1)

            def residual_sum(c):
                dve.wait_ge(s_xb, c + 1)
                for t in range(T):
                    dve.wait_ge(s_c2, T * c + t + 1)
                    dve.tensor_tensor(xs[:, c * CB:(c + 1) * CB, t, :],
                                      bank[6 + t][:, :].rearrange("p (b k) -> p b k", b=CB),
                                      xs[:, c * CB:(c + 1) * CB, t, :], ALU.add).then_inc(s_x1, 1)

            def graphs_low(c, pairs):
                for j in pairs:
                    i = c * PAIRS + j
                    dve.wait_ge(s_xt_hi, i + 1)
                    dve.tensor_tensor(zt_lo[:, 2 * i:2 * i + 2, :].rearrange("k b n -> k (b n)"), xt_bank(c, j)[:, :],
                                      zt_hi[:, 2 * i:2 * i + 2, :].bitcast(F32).rearrange("k b n -> k (b n)"),
                                      ALU.subtract).then_inc(s_xt_lo, 1)

            centre(1, 0)
            variance(1, 0)
            dve.wait_ge(s_ld_l0, 3 * 16)
            dve.wait_ge(s_const, 5)
            dve.tensor_tensor(l0_sum[:, :], l0_raw[:, 2, :], l0_raw[:, 4, :], ALU.add).then_inc(s_w_mix, 1)
            dve.wait_ge(s_w_mix, 1)
            for r in range(2):
                q = slice(r * K, (r + 1) * K)
                dve.tensor_tensor(conv_w[q, 0, q], l0_raw[q, 0, :], l0_sum[q, :], ALU.subtract)
                dve.tensor_tensor(conv_w[q, 1, q], l0_raw[q, 1, :], l0_raw[q, 3, :], ALU.add)
                dve.tensor_scalar(conv_w[q, 2, q], l0_sum[q, :], 2.0, None, ALU.mult).then_inc(s_w_mix, 1)
            centre(1, 1)
            first_norm(0)
            variance(1, 1)
            dve.wait_ge(s_ld_adj, 16)
            for t in range(T):
                last = dve.tensor_scalar(neg_adj[:, t, :].rearrange("p (s q) -> p s q", s=T),
                                         adj_raw[:, t, :].rearrange("p (q s) -> p s q", s=T), -1.0, None, ALU.mult)
            last.then_inc(s_negadj, 1)
            first_norm(1)
            centre(1, 2)
            for c in range(CHUNKS):
                if c + 2 < CHUNKS:
                    variance(1, c + 2)
                residual_sum(c)
                if c != LAST:
                    dve.wait_ge(s_x1, T * (c + 1))
                    centre(2, c)
                if c >= 1:
                    graphs_low(c - 1, range(PAIRS // 2))
                if c + 2 < CHUNKS:
                    first_norm(c + 2)
                if c >= 1:
                    graphs_low(c - 1, range(PAIRS // 2, PAIRS))
                if c != LAST:
                    variance(2, c)
                if c + 3 < CHUNKS:
                    centre(1, c + 3)
                if c != LAST:
                    second_norm(c)
            dve.wait_ge(s_gram_hi, 1)
            part = gram[K:P, :, :].rearrange("p h k -> p (h k)")
            dve.tensor_tensor(part, bank[3][K:P, :], part.bitcast(F32), ALU.subtract).then_inc(s_gram_lo, 1)
            dve.wait_ge(s_w_hi, 1)
            dve.tensor_tensor(head_lo[:, :, :], head_w[:, :, :], head_hi[:, :, :].bitcast(F32), ALU.subtract)\
               .then_inc(s_w_lo, 1)

            def late(b, p):
                if late_slot(b, p) == LATE["centre"]:
                    dve.wait_ge(s_x1, T * CHUNKS)
                    centre(2, LAST)
                if late_slot(b, p) == LATE["variance"]:
                    variance(2, LAST)
                if late_slot(b, p) == LATE["norm"]:
                    second_norm(LAST)
                if late_slot(b, p) in LATE["low"]:
                    graphs_low(LAST, [LATE["low"].index(late_slot(b, p))])

            def weigh(b, p):
                s = at_stage(b, p, "weighted")
                if s is not None:
                    dve.wait_ge(a_sc, s.n)
                    dve.tensor_tensor(u[:, s.at % 3, :, :].rearrange("p t n -> p (t n)"), SC[:, :],
                                      neg_adj[:, :, :].rearrange("p t n -> p (t n)"), ALU.mult).then_inc(a_u, 1)

            def mask(b, p):
                s = at_stage(b, p, "mask")
                if s is not None:
                    dve.wait_ge(a_u, s.n)
                    if s.at_or_later(2):
                        dve.wait_ge(a_nv, s.n - 1)
                    dve.tensor_scalar(msk[:, :, :].rearrange("p t n -> p (t n)"),
                                      u[:, s.at % 3, :, :].rearrange("p t n -> p (t n)"), 0.0, NEG_INF,
                                      ALU.is_equal, ALU.mult).then_inc(a_msk, 1)

            def masked(b, p):
                s = at_stage(b, p, "masked")
                if s is None:
                    return
                dve.wait_ge(a_msk, s.n)
                before = last_in_tile(b, p, "masked")
                if before is not None:
                    dve.wait_ge(a_st, before.n)
                apart(dve)
                for t in range(T):
                    last = dve.tensor_tensor_reduce(nv[:, s.at % 3, t, :], msk[:, t, :], u[:, s.at % 3, t, :], 1.0, 3e38,
                                                    ALU.add, ALU.min, nmax[:, s.at % 3, t:t + 1])
                last.then_inc(a_nv, 1)

            def y_low(b, p):
                s = at_stage(b, p, "y_lo")
                if s is None:
                    return
                if s.is_mix:
                    dve.wait_ge(m_ht_hi, s.mixes)
                    dve.tensor_tensor(m_lo[:, :], m_ht[:, :], m_hi[:, :].bitcast(F32), ALU.subtract)
                    dve.tensor_tensor(m_stack[K:P, :], m_ht[K:P, :], m_hi[K:P, :].bitcast(F32), ALU.subtract)\
                       .then_inc(m_ht_lo, 1)
                    return
                dve.wait_ge(h_y_hi, s.heads)
                dve.tensor_tensor(y[s.other_rows, s.odd, :], Y[s.rows, 0:N], y[s.rows, s.odd, :].bitcast(F32),
                                  ALU.subtract).then_inc(h_y_lo, 1)

            def reciprocal(b, p):
                s = at_stage(b, p, "reciprocal")
                if s is None:
                    return
                dve.wait_ge(a_av, s.n)
                before = last_in_tile(b, p, "reciprocal")
                if before is not None:
                    dve.wait_ge(a_pz, before.n)
                dve.reciprocal(rs[:, s.at % 3, :], AV[:, K:T * (K + 1):K + 1]).then_inc(a_rs, 1)

            def mix_leaky(b, p):
                s = mix_at(b, p, "mix_leaky")
                if s is not None:
                    dve.wait_ge(m_bias, s.mixes)
                    dve.scalar_tensor_tensor(m_l[:, :, :], m_o[:, :, :], SLOPE, m_o[:, :, :],
                                             ALU.mult, ALU.max).then_inc(m_lk, 1)

            def product_low(b, p):
                s = head_at(b, p, "part_lo")
                if s is None:
                    return
                dve.wait_ge(h_pzt_hi, s.heads)
                dve.tensor_tensor(pzt[s.other_rows, s.odd, :], ZT[s.rows, 0:N],
                                  pzt[s.rows, s.odd, :].bitcast(F32), ALU.subtract).then_inc(h_pzt_lo, 1)

            def attend(b):
                for p in range(len(SLOTS)):
                    product_low(b, p)
                    reciprocal(b, p)
                    masked(b, p)
                    weigh(b, p)
                    y_low(b, p)
                    mix_leaky(b, p)
                    mask(b, p)
                    late(b, p)

            rounds(mybir.EngineType.DVE, attend)

        @block.tensor
        def _(pe):
            pe.wait_ge(s_const, 5)
            pe.wait_ge(s_ld_adj, 16)
            for s in range(T):
                for t in range(T):
                    last = pe.transpose(bank[0][:, s * N + t * P:s * N + (t + 1) * P],
                                        adj_raw[:, t, s:N:T], ident[:, :])
            last.then_inc(s_adj_tp, 1)
            pe.wait_ge(s_adj_t, 1)

            def transpose_pairs(c):
                pe.wait_ge(s_hn, c + 1)
                for i in range(2):
                    if c >= 1:
                        pe.wait_ge(s_pt_sb, 2 * (c - 1) + i + 1)
                    if c >= 3:
                        pe.wait_ge(s_xt_lo, PAIRS * (c - 3) + i + 1)
                    for a in range(2):
                        for t in range(T):
                            g = 2 * (2 * i + a)
                            last = pe.transpose(bank[i][:, a * N + t * P:a * N + (t + 1) * P],
                                                hn[:, c % 2, t, g:g + 2, :].rearrange("p b k -> p (b k)"), ident[:, :])
                    last.then_inc(s_pt, 1)

            def weigh_pairs(c, t, out_bank, w, first):
                for a in range(PAIRS):
                    last = pe.matmul(out_bank[:, a * P:(a + 1) * P], pair_t[:, c % 2, a, t * P:(t + 1) * P],
                                     conv_w[:, w, :], start=(first and a == 0), stop=(a == PAIRS - 1),
                                     skip_group_check=True)
                return last

            def diffuse(out_bank, source, t):
                for m in range(T):
                    pe.matmul(out_bank[:, :], adj_t[:, m, t * P:(t + 1) * P], source[:, m, :],
                              start=(m == 0), stop=False, skip_group_check=True)

            def first_product(c):
                pe.wait_ge(s_pt_sb, 2 * (c + 1))
                if c == 0:
                    pe.wait_ge(s_w_mix, 3)
                for t in range(T):
                    if c >= 1:
                        pe.wait_ge(s_cc, T * (c - 1) + t + 1)
                    weigh_pairs(c, t, bank[2 + t], 2, True).then_inc(s_c0, 1)

            def second_product(c):
                pe.wait_ge(s_cc, T * (c + 1))
                for t in range(T):
                    if c >= 1:
                        pe.wait_ge(s_cd, T * (c - 1) + t + 1)
                    diffuse(bank[4 + t], conv_c, t)
                    weigh_pairs(c, t, bank[4 + t], 1, False).then_inc(s_c1, 1)

            def third_product(c):
                pe.wait_ge(s_cd, T * (c + 1))
                for t in range(T):
                    if c >= 1:
                        pe.wait_ge(s_x1, T * (c - 1) + t + 1)
                    if c >= 2:
                        pe.wait_ge(s_xt_lo, PAIRS * (c - 2) + 2 + t + 1)
                    diffuse(bank[6 + t], conv_d, t)
                    weigh_pairs(c, t, bank[6 + t], 0, False).then_inc(s_c2, 1)

            def transpose_graphs(c, pairs):
                pe.wait_ge(s_two, 2 * (c + 1))
                for j in pairs:
                    if c == LAST:
                        pe.wait_ge(s_xt_lo, PAIRS * c + j)
                    else:
                        if j < 2:
                            pe.wait_ge(s_pt_sb, 2 * min(c + 2, CHUNKS - 1) + j + 1)
                        else:
                            pe.wait_ge(s_x1, T * min(c + 1, CHUNKS - 1) + j - 2 + 1)
                        if c >= 1:
                            pe.wait_ge(s_xt_lo, PAIRS * (c - 1) + j + 1)
                    z2 = z_last if c == LAST else z_two[:, c % 2]
                    for a in range(2):
                        for t in range(T):
                            last = pe.transpose(xt_bank(c, j)[:, a * N + t * P:a * N + (t + 1) * P],
                                                z2[:, t, 2 * j + a, :, :].rearrange("p r k -> p (r k)"),
                                                ident[:, :])
                    last.then_inc(s_xt, 1)

            transpose_pairs(0)
            first_product(0)
            for c in range(CHUNKS):
                second_product(c)
                if c == LAST:
                    pe.wait_ge(s_cc, T * CHUNKS)
                    pe.wait_ge(s_ld_w, 6 * 16)
                    for h in range(HEADS):
                        pe.transpose(bank[2][:, h * K:(h + 1) * K], head_w[0:K, h, :], ident[0:K, 0:K])
                    pe.transpose(bank[3][:, 0:HEADS], head_b_rows[:, :], ident[0:HEADS, 0:HEADS]).then_inc(s_wt, 1)
                if c + 1 < CHUNKS:
                    transpose_pairs(c + 1)
                    first_product(c + 1)
                third_product(c)
                if c == LAST:
                    pe.wait_ge(s_wt_sb, 3)
                    for h in range(HEADS):
                        two = head_wt[:, h, :, :].rearrange("d r k -> d (r k)")
                        last = pe.matmul(bank[3][:, h * K:(h + 1) * K], two, head_wt[:, h, 0, :], start=True, stop=True)
                    last.then_inc(s_gram, 1)
                if c >= 1:
                    transpose_graphs(c - 1, range(PAIRS))
            def late(b, p):
                if late_slot(b, p) in LATE["transposed"]:
                    transpose_graphs(LAST, [LATE["transposed"].index(late_slot(b, p))])

            pe.wait_ge(s_xt_lo, PAIRS * LAST)
            pe.wait_ge(s_x1, T * CHUNKS)
            pe.wait_ge(s_gram_lo, 1)
            pe.wait_ge(s_w_lo, 1)
            pe.wait_ge(s_negadj, 1)

            def weights_y(b, p):
                s = head_at(b, p, "y")
                if s is None or s.odd:
                    return
                if s.after(1):
                    pe.wait_ge(h_y_lo, s.heads - 1)
                two = gram[:, s.kind:s.kind + 2, :].rearrange("k h m -> k (h m)")
                for i, part in enumerate((zt_hi, zt_lo)):
                    last = pe.matmul(Y[:, 0:N], two, part[:, bass.ds(s.g, 1), :].rearrange("k b n -> k (b n)"),
                                     start=(i == 0), stop=(i == 1))
                last.then_inc(p_y, 1)

            def scores(b, p):
                s = at_stage(b, p, "scores")
                if s is None:
                    return
                pe.wait_ge(m_ht_lo if s.is_mix else h_y_lo, s.mixes if s.is_mix else s.heads)
                if s.at_or_later(2):
                    pe.wait_ge(a_u, s.n - 1)
                if s.is_mix:
                    apart(pe)
                    for t in range(T):
                        for i, part in enumerate((m_hi, m_lo)):
                            last = pe.matmul(SC[:, t * N:(t + 1) * N], m_stack[:, t * P:(t + 1) * P], part[:, :],
                                             start=(i == 0), stop=(i == 1))
                    last.then_inc(a_sc, 1)
                    pe.wait_ge(s_xt_lo, B // 2)
                    for t in range(T):
                        last = pe.transpose(HV[:, t * K:(t + 1) * K], m_ht[0:K, t * P:(t + 1) * P], ident[0:K, 0:K])
                    last.then_inc(m_tr, 1)
                    return
                for t in range(T):
                    for i, part in enumerate((zt_hi, zt_lo)):
                        last = pe.matmul(SC[:, t * N:(t + 1) * N], y[:, s.odd, t * P:(t + 1) * P],
                                         part[:, bass.ds(s.g, 1), :].rearrange("k b n -> k (b n)"),
                                         start=(i == 0), stop=(i == 1))
                last.then_inc(a_sc, 1)

            def transpose(b, p):
                s = at_stage(b, p, "transposed")
                if s is None:
                    return
                pe.wait_ge(a_dd, s.n)
                if s.at_or_later(2):
                    pe.wait_ge(a_pt, s.n - 1)
                for col in range(T):
                    for t in range(T):
                        last = pe.transpose(ST[:, col * N + t * P:col * N + (t + 1) * P],
                                            nv[:, s.at % 3, t, col * P:(col + 1) * P], ident[:, :])
                last.then_inc(a_st, 1)

            def apply(b, p):
                s = at_stage(b, p, "applied")
                if s is None:
                    return
                pe.wait_ge(a_pt, s.n)
                if s.is_mix:
                    pe.wait_ge(m_hv_sb, s.mixes)
                if s.at_or_later(2):
                    pe.wait_ge(a_pz, s.n - 1)
                for t in range(T):
                    for m in range(T):
                        val = m_hv[:, m, :] if s.is_mix else z[:, bass.ds(s.g, 1), m, :].rearrange("p b k -> p (b k)")
                        last = pe.matmul(AV[:, t * (K + 1):(t + 1) * (K + 1)], pt[:, s.at % 3, m, t * P:(t + 1) * P],
                                         val, start=(m == 0), stop=(m == T - 1))
                last.then_inc(a_av, 1)

            def transpose_back(b, p):
                s = head_at(b, p, "back")
                if s is None or not s.odd:
                    return
                pe.wait_ge(a_pz, s.n)
                if s.after(2):
                    pe.wait_ge(h_pzt_lo, s.heads - 2)
                for t in range(T):
                    last = pe.transpose(ZT[:, t * P:(t + 1) * P],
                                        pz[:, s.half, t, :, :].rearrange("p h k -> p (h k)"), ident[:, :])
                last.then_inc(p_zt, 1)

            def project(b, p):
                s = head_at(b, p, "projected")
                if s is None:
                    return
                pe.wait_ge(h_pzt_lo, s.heads)
                if s.after(1):
                    pe.wait_ge(h_cat, s.heads - 1)
                for i, part in enumerate((head_hi, head_lo)):
                    last = pe.matmul(CT[:, 0:N], part[:, s.kind, :], pzt[:, s.odd, :],
                                     start=(i == 0), stop=(i == 1))
                last.then_inc(h_ct, 1)

            def project_out(b, p):
                s = head_at(b, p, "out")
                if s is None:
                    return
                pe.wait_ge(h_lk, s.heads)
                if s.kind == 0 and s.after(1):
                    pe.wait_ge(m_ht_sb, s.g)
                two = out_w[:, s.kind, :, :].rearrange("d r k -> d (r k)")
                pe.matmul(WO[:, 0:N], two, cat[:, s.odd, :], start=(s.kind == 0),
                          stop=(s.kind == HEADS - 1), skip_group_check=True).then_inc(h_wo, 1)

            def attend(b):
                for p in range(len(SLOTS)):
                    scores(b, p)
                    transpose(b, p)
                    project(b, p)
                    transpose_back(b, p)
                    apply(b, p)
                    project_out(b, p)
                    weights_y(b, p)
                    late(b, p)

            rounds(mybir.EngineType.PE, attend)


_INS = ["x", "adj", "L0_gnn_weight", "L0_gnn_bias", "L1_gnn_Wh", "L1_gnn_bh", "L1_gnn_W_out", "L1_gnn_b_out"]
_OUTS = [((32, 256, 64), "float32")]


def kernel(**inputs):
    import numpy as _np
    import concourse.bacc as _bacc
    from concourse import mybir as _mybir
    from concourse.bass_utils import run_bass_kernel_spmd as _run

    nc = _bacc.Bacc("TRN2", target_bir_lowering=False, num_devices=1)
    arrays, args = {}, []
    for name in _INS:
        a = _np.ascontiguousarray(inputs[name])
        arrays[f"in_{name}_dram"] = a
        args.append(nc.dram_tensor(f"in_{name}_dram", a.shape, _mybir.dt.from_np(a.dtype), kind="ExternalInput").ap())
    for i, (shape, dtype) in enumerate(_OUTS):
        dt = _mybir.dt.from_np(_np.dtype(dtype))
        args.append(nc.dram_tensor(f"out_{i}_dram", shape, dt, kind="ExternalOutput").ap())
    graph_block(nc, *args)
    r = _run(nc, [arrays], core_ids=[0])
    got = tuple(r.results[0][f"out_{i}_dram"] for i in range(len(_OUTS)))
    return got[0]
```
